# Optimizing a Trainium2 kernel written in Bass

```python
import numpy as np
import jax
import jax.numpy as jnp

def _softmax(x, axis=-1):
    return jax.nn.softmax(x, axis=axis)

def _gelu(x):
    return jax.nn.gelu(x, approximate=True)

def _silu(x):
    return jax.nn.silu(x)

def _sigmoid(x):
    return jax.nn.sigmoid(x)

def _layernorm(x, axis=-1, eps=1e-05):
    m = jnp.mean(x, axis=axis, keepdims=True)
    v = jnp.var(x, axis=axis, keepdims=True)
    return (x - m) / jnp.sqrt(v + eps)

def _scatter_add(tgt, idx, src, axis=0):
    return tgt.at[idx].add(src)

def _segment_sum(src, seg, n):
    return jax.ops.segment_sum(src, seg, n)
kernel_name = 'mk_adj_ffn_d1_adj_r2_255d7b'

def setup_inputs(seed: int=0):
    np.random.seed(seed)
    _w = jnp.asarray

    def _rec_inputs():
        import jax
        import jax.numpy as jnp
        _gk = jax.random.key(seed)
        x = -0.0002928 + 1 * jax.random.normal(jax.random.fold_in(_gk, 1), (3327, 128), jnp.float32)
        _w = (1.0 + jnp.arange(3327, dtype=jnp.float32)) ** (-0.5)
        _w = _w / _w.mean()
        _pij = jnp.clip(0.00961827 * _w[:, None] * _w[None, :], 0.0, 1.0)
        _a = jax.random.uniform(jax.random.fold_in(_gk, 2), (3327, 3327)) < _pij
        adj = _a.astype(jnp.int32)
        return (x, adj)
    x, adj = _rec_inputs()

    def _L0_gnn_setup():
        import jax, jax.numpy as jnp
        import numpy as np
        N = 8192
        D = 128
        key = jax.random.key(seed)
        k1, k2, k3, k4 = jax.random.split(key, 4)
        x = jax.random.normal(k1, (N, D), dtype=jnp.float32)
        adj = jax.random.randint(k2, (N, N), 0, 2, dtype=jnp.int32)
        W = jax.random.normal(k3, (D, D), dtype=jnp.float32) * 0.05
        b = jax.random.normal(k4, (D,), dtype=jnp.float32) * 0.05
        return {'x': x, 'adj': adj, 'W': W, 'b': b}
    _L0_gnn_all = _L0_gnn_setup()
    _L0_gnn_in = {k: v for k, v in _L0_gnn_all.items() if k in ('W', 'b')}
    del _L0_gnn_all

    def _L0_ffn_setup():
        import jax, jax.numpy as jnp
        import numpy as np
        D_MODEL = 128
        N_EXPERTS = 16
        HIDDEN = 256
        SCALE = 0.02
        key = jax.random.key(seed)
        ks = jax.random.split(key, 5)
        x = jax.random.normal(ks[0], (4, 4096, D_MODEL), dtype=jnp.float32)
        gate_w = jax.random.normal(ks[1], (D_MODEL, N_EXPERTS), dtype=jnp.float32) * SCALE
        gate_b = jnp.zeros((N_EXPERTS,), dtype=jnp.float32)
        w1 = jax.random.normal(ks[2], (N_EXPERTS, D_MODEL, HIDDEN), dtype=jnp.float32) * SCALE
        w2 = jax.random.normal(ks[3], (N_EXPERTS, D_MODEL, HIDDEN), dtype=jnp.float32) * SCALE
        w3 = jax.random.normal(ks[4], (N_EXPERTS, HIDDEN, D_MODEL), dtype=jnp.float32) * SCALE
        return {'x': x, 'gate_w': gate_w, 'gate_b': gate_b, 'w1': w1, 'w2': w2, 'w3': w3}
    _L0_ffn_all = _L0_ffn_setup()
    _L0_ffn_in = {k: v for k, v in _L0_ffn_all.items() if k in ('gate_w', 'gate_b', 'w1', 'w2', 'w3')}
    del _L0_ffn_all
    return {'x': x, 'adj': adj, 'L0_gnn_W': _L0_gnn_in['W'], 'L0_gnn_b': _L0_gnn_in['b'], 'L0_ffn_gate_w': _L0_ffn_in['gate_w'], 'L0_ffn_gate_b': _L0_ffn_in['gate_b'], 'L0_ffn_w1': _L0_ffn_in['w1'], 'L0_ffn_w2': _L0_ffn_in['w2'], 'L0_ffn_w3': _L0_ffn_in['w3']}

def reference(x, adj, L0_gnn_W, L0_gnn_b, L0_ffn_gate_w, L0_ffn_gate_b, L0_ffn_w1, L0_ffn_w2, L0_ffn_w3):
    import jax
    import jax.numpy as jnp

    def _L0_gnn_ref(x, adj, W, b):
        import jax, jax.numpy as jnp
        import numpy as np
        N = 8192
        D = 128
        a = (adj == 1).astype(x.dtype)
        deg = jnp.sum(a, axis=1, keepdims=True)
        agg = jnp.einsum('ij,jf->if', a, x) / deg
        return agg @ W.T + b

    def _L0_ffn_ref(x, gate_w, gate_b, w1, w2, w3):
        import jax, jax.numpy as jnp
        import numpy as np
        D_MODEL = 128
        N_EXPERTS = 16
        HIDDEN = 256
        SCALE = 0.02
        n_experts = w1.shape[0]
        logits = jnp.einsum('bsd,de->bse', x, gate_w) + gate_b
        probs = jax.nn.softmax(logits, axis=-1)
        top_probs, top_idx = jax.lax.top_k(probs, 2)
        top_probs = top_probs / jnp.sum(top_probs, axis=-1, keepdims=True)
        dispatch = jnp.sum(jax.nn.one_hot(top_idx, n_experts, dtype=x.dtype) * top_probs[..., None], axis=-2)
        h1 = jnp.einsum('bsd,edh->bseh', x, w1)
        h2 = jnp.einsum('bsd,edh->bseh', x, w2)
        hidden = jax.nn.silu(h1) * h2
        expert_out = jnp.einsum('bseh,eho->bseo', hidden, w3)
        return jnp.einsum('bseo,bse->bso', expert_out, dispatch)
    x = x + _L0_gnn_ref(_layernorm(x, axis=-1), adj, L0_gnn_W, L0_gnn_b)
    x = x + _L0_ffn_ref(_layernorm(x, axis=-1)[None], L0_ffn_gate_w, L0_ffn_gate_b, L0_ffn_w1, L0_ffn_w2, L0_ffn_w3)[0]
    return x

_drawn_inputs = setup_inputs


def setup_inputs(seed=0):
    import zlib

    import numpy as np

    out = dict(_drawn_inputs(seed))
    spreads = {'L0_ffn_gate_b': (0.0, 0.8)}
    factors = {'L0_ffn_gate_w': 8.0, 'L0_ffn_w1': 8.0, 'L0_ffn_w2': 8.0, 'L0_ffn_w3': 8.0}
    for name, (base, spread) in spreads.items():
        noise = np.random.default_rng([zlib.crc32(name.encode()), seed]).standard_normal(out[name].shape)
        drawn = base * np.exp(spread * noise) if base else spread * noise
        out[name] = jnp.asarray(drawn.astype(out[name].dtype))
    for name, factor in factors.items():
        out[name] = (out[name] * factor).astype(out[name].dtype)
    return out
```

```python
from contextlib import ExitStack

import numpy as np
import concourse.bass as bass
from concourse import mybir

P = 128
D = 128
E = 16
H = 256
EPS = 1e-5
XSCALE = 4096.0
XPW = 264
ROW = 132
DEST, WEIGHT = 128, 129
NOWHERE = 1 << 20
ROUNDER = 12582912.0
JH = 2


def adj_ffn(nc, x, adj, wt, gnn_b, gate_w, gate_b, w1, w2, w3, out):
    f32, f16, bf16, i32, u32 = (mybir.dt.float32, mybir.dt.float16, mybir.dt.bfloat16,
                                mybir.dt.int32, mybir.dt.uint32)
    ALU, ACT, AX = mybir.AluOpType, mybir.ActivationFunctionType, mybir.AxisListType

    T = x.shape[1] // D
    JT = T // JH
    PAIRS = T // 2
    BOUND = T * P * 2 - 1
    BLOCKS = (T * P * 2 + E * (P - 1)) // P
    BLOCKS += -BLOCKS % 4
    REGION = T * P + P
    TRASH = E * REGION
    DUMMY = TRASH + P
    ROWS = DUMMY + P
    n_tokens = out.shape[0]
    CHUNKS = [(a, min(a + 7, T)) for a in range(0, T, 7)]
    CONSTS = 22

    routed = nc.dram_tensor("routed_rows", [ROWS, ROW], f32).ap()
    returned = nc.dram_tensor("returned_rows", [T * P * 2, D], f32).ap()

    ctx = ExitStack()
    with ctx:
        def sb(name, shape, dt):
            return ctx.enter_context(nc.sbuf_tensor(name, shape, dt))

        def bank(name):
            return ctx.enter_context(nc.psum_tensor(name, [P, 512], f32))

        sems = {}

        BY_BUFFER = {"adj_loaded", "converted", "routed_0", "routed_1", "dest_ready", "xT_done", "ticket_ready",
                     "block_loaded", "y_returned", "back_loaded"}

        def S(name, b=""):
            key = f"{name}{b}" if name in BY_BUFFER else name
            if key not in sems:
                sems[key] = ctx.enter_context(nc.semaphore(key))
            return sems[key]

        x_in = sb("x_in", [P, T, D], f32)
        w12 = sb("w12", [P, E * 2 * H], f32)
        w3s = sb("w3s", [P, E * H], f32)
        wt_s = sb("wt_s", [P, D], f32)
        gw_s = sb("gw_s", [P, E], f32)
        gb_s = sb("gb_s", [1, E], f32)
        b_rows = sb("b_rows", [P, D], f32)
        ident = sb("ident", [P, P], f32)
        tri = sb("tri", [P, P], bf16)
        ones = sb("ones", [P, P], bf16)
        onesf = sb("onesf", [P, P], f32)
        tri16 = sb("tri16", [E, E], f32)
        iota_e = sb("iota_e", [P, E], f32)
        base_tok = sb("base_tok", [P, E], f32)
        trash = sb("trash", [P, 1], f32)
        exponent = sb("exponent", [P, T], f32)
        e_col = sb("e_col", [E, 1], f32)
        base_col = sb("base_col", [E, 1], f32)
        iota_n = sb("iota_n", [E, BLOCKS], f32)
        iota_n128 = sb("iota_n128", [E, BLOCKS], f32)
        region_row = sb("region_row", [1, E], f32)
        filler = sb("filler", [P, ROW], f32)
        stats = sb("stats", [P, T, 6], f32)
        m_sum = sb("m_sum", [P, T], f32)
        m_dif = sb("m_dif", [P, T], f32)
        m_dif2 = sb("m_dif2", [P, T], f32)
        v_sum = sb("v_sum", [P, T], f32)
        v_eps = sb("v_eps", [P, T], f32)
        v_all = sb("v_all", [P, T], f32)
        mean1 = sb("mean1", [P, T], f32)
        rstd0 = sb("rstd0", [P, T], f32)
        rstd1 = sb("rstd1", [P, T], f32)
        xn = sb("xn", [P, T, D], f32)
        xp = sb("xp", [P, T, XPW], f16)
        two = range(2)
        adj32 = [[sb(f"adj32_{b}{h}", [P, JT * P], i32) for h in range(JH)] for b in two]
        a16 = [sb(f"a16_{b}", [P, T * P], f16) for b in two]
        rdeg = [sb(f"rdeg{b}", [P, 1], f32) for b in two]
        lo_part = [sb(f"lo_part{b}", [P, D], f32) for b in two]
        agg = [sb(f"agg{b}", [P, D], f32) for b in two]
        aggT = [sb(f"aggT{b}", [P, D], f32) for b in two]
        x1 = [sb(f"x1_{b}", [P, D], f32) for b in two]
        x1_all = sb("x1_all", [P, T, D], f32)
        st2 = [sb(f"st2_{b}", [P, 6], f32) for b in two]
        mv2 = [sb(f"mv2_{b}", [P, 2], f32) for b in two]
        ve2 = [sb(f"ve2_{b}", [P, 1], f32) for b in two]
        rstd2 = [sb(f"rstd2_{b}", [P, 1], f32) for b in two]
        row = [[sb(f"row{b}{k}", [P, ROW], f32) for k in two] for b in two]
        ynT = [sb(f"ynT{b}", [P, D], f32) for b in two]
        neg_max = [sb(f"neg_max{b}", [P, 1], f32) for b in two]
        expo = [sb(f"expo{b}", [P, E], f32) for b in two]
        exp_sum = [sb(f"exp_sum{b}", [P, 1], f32) for b in two]
        rsum = sb("rsum", [P, 1], f32)
        probs = sb("probs", [P, E], f32)
        top8 = sb("top8", [P, 8], f32)
        idx8 = sb("idx8", [P, 8], u32)
        idxf = sb("idxf", [P, 2], f32)
        den = sb("den", [P, 1], f32)
        rden = sb("rden", [P, 1], f32)
        onehot = [sb(f"onehot{k}", [P, E], f32) for k in two]
        mask = sb("mask", [P, E], bf16)
        mask_sum = sb("mask_sum", [P, E], bf16)
        place = sb("place", [P, E], f32)
        picked = [sb(f"picked{k}", [P, E], f32) for k in two]
        posf = sb("posf", [P, 2], f32)
        pos = [sb(f"pos{b}", [P, 2], i32) for b in two]
        full0 = sb("full0", [E, 1], f32)
        full = sb("full", [E, 1], f32)
        full_prev = sb("full_prev", [E, 1], f32)
        new = sb("new", [E, 1], f32)
        seq = sb("seq", [E, 1], f32)
        end = sb("end", [E, 1], f32)
        lag = sb("lag", [E, 1], f32)
        off = sb("off", [E, 1], f32)
        since = sb("since", [E, BLOCKS], f32)
        holds = sb("holds", [E, BLOCKS], f32)
        offs = sb("offs", [E, BLOCKS], f32)
        tabf = sb("tabf", [1, 2 * BLOCKS], f32)
        tab = sb("tab", [1, 2 * BLOCKS], i32)
        endf = sb("endf", [1, E], f32)
        endi = sb("endi", [1, E], i32)
        four = range(4)
        xblk = [sb(f"xblk{b}", [P, ROW], f32) for b in four]
        ticket = [sb(f"ticket{b}", [P, 2], f32) for b in four]
        xT = [sb(f"xT{b}", [P, P], f32) for b in two]
        th = [sb(f"th{b}", [P, H], f32) for b in two]
        gated = [sb(f"gated{b}", [P, H], f32) for b in two]
        hid = [sb(f"hid{b}", [P, H], f32) for b in two]
        hidT = [sb(f"hidT{b}", [P, H], f32) for b in two]
        yblk = [sb(f"yblk{b}", [P, D], f32) for b in four]
        back = sb("back", [P, T, 2 * D], f32)

        psA = [bank(f"psA{b}") for b in two]
        psH = [bank(f"psH{b}") for b in two]
        psHT = bank("psHT")
        psXY = bank("psXY")
        psT = bank("psT")
        psG = bank("psG")

        block = ctx.enter_context(nc.Block())


        def item(i, b, back, period):
            return (i, b - back) if b >= back else item(i - 1, b + period, back, period)

        def after(eng, name, i, b, back=0, period=2):
            i, b = item(i, b, back, period)
            if not (isinstance(i, int) and i < 0):
                eng.wait_ge(S(name, b), i + 1 if name in BY_BUFFER else period * i + b + 1)

        def apart(eng):
            eng.nop(nofuse=True)

        def tile_pipeline(eng, step):
            def run(i, b):
                s = 2 * i + b if isinstance(i, int) else None
                on = [s is None or 0 <= s - back < T for back in range(4)]
                step(i, b, *on)
            for s in range(4):
                run(s // 2, s % 2)
            with eng.Fori(2, PAIRS) as i:
                run(i, 0)
                run(i, 1)
            for s in range(T, T + 3):
                run(s // 2, s % 2)

        def block_pipeline(eng, step):
            def run(i, b):
                s = 4 * i + b if isinstance(i, int) else None
                on = [s is None or 0 <= s - back < BLOCKS for back in range(4)]
                step(i, b, *on)
            for s in range(4):
                run(0, s)
            with eng.Fori(1, BLOCKS // 4) as i:
                for b in four:
                    run(i, b)
            for s in range(BLOCKS, BLOCKS + 3):
                run(s // 4, s % 4)

        @block.sync
        def _(sp):
            sp.dma_start(x_in[:, :, :], x.rearrange("p (t d) -> p t d", d=D)).then_inc(S("x_loaded"), 16)
            sp.dma_start(b_rows[:, :], gnn_b.partition_broadcast(P)).then_inc(S("b_loaded"), 16)
            sp.dma_start(wt_s[:, :], wt).then_inc(S("wt_loaded"), 16)
            sp.dma_start(gw_s[:, :], gate_w).then_inc(S("gw_loaded"), 16)
            sp.dma_start(gb_s[:, :], gate_b.rearrange("(a e) -> a e", a=1)).then_inc(S("gb_loaded"), 16)

            def load_adjacency(i):
                for b in two:
                    for h in range(JH):
                        if not isinstance(i, int):
                            sp.wait_ge(S("converted", f"{b}{h}"), i)
                        sp.dma_start(adj32[b][h][:, :], adj[2 * i + b, :, h * JT * P:(h + 1) * JT * P])\
                            .then_inc(S("adj_loaded", f"{b}{h}"), 16)

            load_adjacency(0)
            with sp.Fori(1, PAIRS) as i:
                load_adjacency(i)
            sp.wait_ge(S("tab_ready"), 1)
            sp.wait_ge(S("tails_filled"), 16 * E)
            sp.wait_ge(S("dummy_filled"), 16)
            for b in two:
                sp.wait_ge(S("routed_0", b), 16 * PAIRS)
                sp.wait_ge(S("routed_1", b), 16 * PAIRS)

            def load_blocks(i):
                for b in four:
                    first = sp.value_load(tab[0:1, bass.ds(4 * i + b, 1)], min_val=0, max_val=DUMMY)
                    if not isinstance(i, int):
                        sp.wait_ge(S("xT_done", b), i)
                        sp.wait_ge(S("ticket_ready", b), i)
                    sp.dma_start(xblk[b][:, :], routed[bass.ds(first, P), :]).then_inc(S("block_loaded", b), 16)

            load_blocks(0)
            with sp.Fori(1, BLOCKS // 4) as i:
                load_blocks(i)
            for b in four:
                sp.wait_ge(S("y_returned", b), 16 * (BLOCKS // 4))
            pairs = returned.rearrange("(t p k) d -> p t (k d)", p=P, k=2)
            for c, (a, z) in enumerate(CHUNKS):
                sp.dma_start(back[:, a:z, :], pairs[:, a:z, :]).then_inc(S("back_loaded", c), 16)
            whole = n_tokens // P
            for c, (a, z) in enumerate(CHUNKS):
                sp.wait_ge(S("combined"), c + 1)
                z = min(z, whole)
                sp.dma_start(out[a * P:z * P, :].rearrange("(t p) d -> p t d", p=P), xn[:, a:z, :])\
                    .then_inc(S("out_stored"), 16)
            left = n_tokens - whole * P
            sp.dma_start(out[whole * P:n_tokens, :], xn[0:left, whole, :]).then_inc(S("out_stored"), 16)
            sp.wait_ge(S("out_stored"), 16 * (len(CHUNKS) + 1))

        @block.scalar
        def _(act):
            for e in range(E):
                act.dma_start(w12[:, e * 2 * H:e * 2 * H + H], w1[e]).then_inc(S("weights_loaded"), 16)
                act.dma_start(w12[:, e * 2 * H + H:(e + 1) * 2 * H], w2[e]).then_inc(S("weights_loaded"), 16)
                act.dma_start(w3s[:, e * H:(e + 1) * H].rearrange("p (c n) -> p c n", c=2),
                              w3[e].rearrange("(c p) n -> p c n", p=P)).then_inc(S("weights_loaded"), 16)
            act.wait_ge(S("xn_ready"), 1)
            nc.scalar.activation(xp[:, :, 0:D], xn[:, :, :], ACT.Copy).then_inc(S("xp_high"), 1)

            def step(i, b, convert, aggregate, front, route):
                fi, fb = item(i, b, 2, 2)
                if front:
                    after(act, "rdeg_ready", i, b, 2)
                    after(act, "agg_ready", i, b, 4)
                    nc.scalar.activation(lo_part[fb][:, :], psA[fb][:, D:2 * D], ACT.Copy,
                                         scale=rdeg[fb][:, 0:1]).then_inc(S("lo_ready", fb), 1)
                    after(act, "aggT_done", i, b, 2)
                    after(act, "gnn_done", i, b, 4)
                    nc.scalar.activation(aggT[fb][:, :], psT[:, 0:P], ACT.Copy).then_inc(S("aggT_ready", fb), 1)
                if route:
                    ri, rb = item(i, b, 3, 2)
                    after(act, "max_ready", i, b, 3)
                    after(act, "mask_ready", i, b, 5)
                    nc.scalar.activation(expo[rb][:, :], psG[:, 0:E], ACT.Exp, bias=neg_max[rb][:, 0:1],
                                         accum_out=exp_sum[rb][:, 0:1]).then_inc(S("exp_ready", rb), 1)
                if front:
                    after(act, "x1_ready", i, b, 2)
                    nc.scalar.activation(x1_all[:, 2 * fi + fb, :], x1[fb][:, :], ACT.Copy)\
                        .then_inc(S("x1_kept", fb), 1)
                    after(act, "ynT_done", i, b, 2)
                    after(act, "logits_done", i, b, 4)
                    nc.scalar.activation(ynT[fb][:, :], psT[:, 0:P], ACT.Copy).then_inc(S("ynT_ready", fb), 1)

            tile_pipeline(act, step)

            act.wait_ge(S("ends_ready"), 1)
            act.wait_ge(S("filler_ready"), 1)
            for e in range(E):
                first = act.value_load(endi[0:1, e:e + 1], min_val=0, max_val=TRASH - P)
                act.dma_start(routed[bass.ds(first, P), :], filler[:, :]).then_inc(S("tails_filled"), 16)

            def block_step(i, b, start, first, middle, last):
                if start:
                    after(act, "xT_done", i, b, 0, 4)
                    after(act, "h_done", i, b, 2, 4)
                    nc.scalar.activation(xT[b % 2][:, :], psXY[:, 0:P], ACT.Copy).then_inc(S("xT_ready", b), 1)
                if first:
                    fb = item(i, b, 1, 4)[1]
                    after(act, "h_done", i, b, 1, 4)
                    after(act, "hid_ready", i, b, 3, 4)
                    nc.scalar.activation(th[fb % 2][:, :], psH[fb % 2][:, 0:H], ACT.Tanh, scale=0.5)\
                        .then_inc(S("th_ready", fb), 1)
                if last:
                    lb = item(i, b, 3, 4)[1]
                    after(act, "y_done", i, b, 3, 4)
                    after(act, "ticket_ready", i, b, 3, 4)
                    nc.scalar.activation(yblk[lb][:, :], psXY[:, P:2 * P], ACT.Copy,
                                         scale=ticket[lb][:, 1:2]).then_inc(S("y_ready", lb), 1)
                if middle:
                    mb = item(i, b, 2, 4)[1]
                    after(act, "hidT_done", i, b, 2, 4)
                    after(act, "y_done", i, b, 4, 4)
                    nc.scalar.activation(hidT[mb % 2][:, :], psHT[:, 0:H], ACT.Copy).then_inc(S("hidT_ready", mb), 1)

            block_pipeline(act, block_step)

        @block.gpsimd
        def _(pool):
            g = nc.gpsimd
            big = dict(allow_small_or_imprecise_dtypes=True)
            g.memset(exponent[:, :], -0.5).then_inc(S("exponent_ready"), 1)
            g.memset(ident[:, :], 0.0).then_inc(S("const_memset"), 1)
            g.memset(tri[:, :], 1.0).then_inc(S("const_memset"), 1)
            g.memset(tri16[:, :], 1.0).then_inc(S("const_memset"), 1)
            g.memset(filler[:, :], 0.0).then_inc(S("const_memset"), 1)
            for b in two:
                for k in two:
                    g.memset(row[b][k][:, :], 0.0).then_inc(S("const_memset"), 1)
            pool.wait_ge(S("const_memset"), 8)
            g.affine_select(out=ident[:, :], in_=ident[:, :], compare_op=ALU.not_equal, fill=1.0, base=0,
                            pattern=[[-1, P]], channel_multiplier=1).then_inc(S("const_ready"), 1)
            for m, n in ((tri, P), (tri16, E)):
                g.affine_select(out=m[:, :], in_=m[:, :], compare_op=ALU.is_gt, fill=0.0, base=0,
                                pattern=[[1, n]], channel_multiplier=-1).then_inc(S("const_ready"), 1)
            g.memset(filler[:, DEST:DEST + 1].bitcast(i32), NOWHERE).then_inc(S("filler_ready"), 1)
            for b in two:
                for k in two:
                    g.iota(row[b][k][:, DEST:DEST + 1].bitcast(i32), pattern=[[0, 1]], base=2 * P * b + k,
                           channel_multiplier=2).then_inc(S("const_ready"), 1)
            g.memset(ones[:, :], 1.0).then_inc(S("const_ready"), 1)
            g.memset(onesf[:, :], 1.0).then_inc(S("const_ready"), 1)
            g.memset(mask_sum[:, :], 0.0).then_inc(S("const_ready"), 1)
            g.memset(full_prev[:, :], 0.0).then_inc(S("const_ready"), 1)
            g.memset(tabf[:, 0:BLOCKS], float(DUMMY)).then_inc(S("const_ready"), 1)
            g.memset(tabf[:, BLOCKS:2 * BLOCKS], 0.0).then_inc(S("const_ready"), 1)
            g.memset(xp[:, :, 2 * D:2 * D + 1], XSCALE).then_inc(S("const_ready"), 1)
            g.iota(iota_e[:, :], pattern=[[1, E]], base=0, channel_multiplier=0, **big).then_inc(S("const_ready"), 1)
            g.iota(base_tok[:, :], pattern=[[REGION, E]], base=-TRASH, channel_multiplier=-1, **big)\
                .then_inc(S("const_ready"), 1)
            g.iota(trash[:, :], pattern=[[0, 1]], base=TRASH, channel_multiplier=1, **big)\
                .then_inc(S("const_ready"), 1)
            g.iota(e_col[:, :], pattern=[[0, 1]], base=0, channel_multiplier=1, **big)\
                .then_inc(S("const_ready"), 1)
            g.iota(base_col[:, :], pattern=[[0, 1]], base=-DUMMY, channel_multiplier=REGION, **big)\
                .then_inc(S("const_ready"), 1)
            g.iota(iota_n[:, :], pattern=[[1, BLOCKS]], base=0, channel_multiplier=0, **big)\
                .then_inc(S("const_ready"), 1)
            g.iota(iota_n128[:, :], pattern=[[P, BLOCKS]], base=0, channel_multiplier=0, **big)\
                .then_inc(S("const_ready"), 1)
            g.iota(region_row[:, :], pattern=[[REGION, E]], base=0, channel_multiplier=0, **big)\
                .then_inc(S("const_ready"), 1)
            pool.wait_ge(S("filler_ready"), 1)
            pool.dma_start(routed[DUMMY:DUMMY + P, :], filler[:, :]).then_inc(S("dummy_filled"), 16)
            pool.wait_ge(S("v_ready"), 1)
            pool.wait_ge(S("exponent_ready"), 1)
            g.tensor_tensor(rstd0[:, :], v_all[:, :], exponent[:, :], ALU.pow).then_inc(S("rstd0_ready"), 1)
            pool.wait_ge(S("xn_ready"), 1)
            pool.wait_ge(S("b_loaded"), 16)
            g.tensor_tensor(x_in[:, :, :], x_in[:, :, :], b_rows[:, None, :].broadcast_to([P, T, D]), ALU.add)\
                .then_inc(S("xb_ready"), 1)

            def step(i, b, convert, aggregate, front, route):
                if front:
                    fi, fb = item(i, b, 2, 2)
                    after(pool, "ve_ready", i, b, 2)
                    g.tensor_tensor(rstd2[fb][:, :], ve2[fb][:, :], exponent[:, 0:1], ALU.pow)\
                        .then_inc(S("rstd2_ready", fb), 1)
                    if not (isinstance(fi, int) and fi == 0):
                        for k in two:
                            pool.wait_ge(S(f"routed_{k}", fb), 16 * fi)
                            apart(pool)
                            dest = row[fb][k][:, DEST:DEST + 1].bitcast(i32)
                            g.tensor_scalar(dest, dest, 4.0 * P, None, ALU.add).then_inc(S("dest_ready", fb), 1)
                    after(pool, "yn_ready", i, b, 2)
                    apart(pool)
                    g.tensor_copy(row[fb][1][:, 0:D], row[fb][0][:, 0:D]).then_inc(S("yn_copied", fb), 1)
                if route:
                    ri, rb = item(i, b, 3, 2)
                    after(pool, "pos_ready", i, b, 3)
                    after(pool, "yn_copied", i, b, 3)
                    if not (isinstance(ri, int) and ri == 0):
                        pool.wait_ge(S("dest_ready", rb), 2 * ri)
                    apart(pool)
                    for k in two:
                        g.indirect_dma_start(routed[:, :], bass.IndirectOffsetOnAxis(pos[rb][:, k:k + 1], 0),
                                             row[rb][k][:, :], None).then_inc(S(f"routed_{k}", rb), 16)

            pool.wait_ge(S("const_ready"), CONSTS)
            tile_pipeline(pool, step)

            def block_step(i, b, start, first, middle, last):
                if start:
                    pool.wait_ge(S("block_loaded", b), 16 * i + 16)
                    if not (isinstance(i, int) and i == 0):
                        pool.wait_ge(S("y_returned", b), 16 * i)
                    apart(pool)
                    g.tensor_copy(ticket[b][:, :], xblk[b][:, DEST:DEST + 2]).then_inc(S("ticket_ready", b), 1)
                if last:
                    li, lb = item(i, b, 3, 4)
                    after(pool, "ticket_ready", i, b, 3, 4)
                    after(pool, "y_ready", i, b, 3, 4)
                    apart(pool)
                    g.indirect_dma_start(returned[:, :],
                                         bass.IndirectOffsetOnAxis(ticket[lb][:, 0:1].bitcast(i32), 0),
                                         yblk[lb][:, :], None, bounds_check=BOUND, oob_is_err=False)\
                        .then_inc(S("y_returned", lb), 16)

            block_pipeline(pool, block_step)

        @block.vector
        def _(dve):
            v = nc.vector

            def then(ins, name, b=""):
                ins.then_inc(S(name, b), 1)

            dve.wait_ge(S("x_loaded"), 16)
            for t in range(T):
                last = v.bn_stats(stats[:, t, :], x_in[:, t, :])
            last.then_inc(S("stats_ready"), 1)
            dve.wait_ge(S("stats_ready"), 1)
            v.tensor_tensor(m_sum[:, :], stats[:, :, 1], stats[:, :, 4], ALU.add).then_inc(S("m_ready"), 1)
            v.tensor_tensor(m_dif[:, :], stats[:, :, 1], stats[:, :, 4], ALU.subtract).then_inc(S("m_ready"), 1)
            v.tensor_tensor(v_sum[:, :], stats[:, :, 2], stats[:, :, 5], ALU.add).then_inc(S("m_ready"), 1)
            dve.wait_ge(S("m_ready"), 3)
            v.tensor_scalar(mean1[:, :], m_sum[:, :], 0.5, None, ALU.mult).then_inc(S("m2_ready"), 1)
            v.tensor_tensor(m_dif2[:, :], m_dif[:, :], m_dif[:, :], ALU.mult).then_inc(S("m2_ready"), 1)
            v.tensor_scalar(v_eps[:, :], v_sum[:, :], 1.0 / D, EPS, ALU.mult, ALU.add).then_inc(S("m2_ready"), 1)
            dve.wait_ge(S("m2_ready"), 3)
            v.scalar_tensor_tensor(v_all[:, :], m_dif2[:, :], 0.25, v_eps[:, :], ALU.mult, ALU.add)\
                .then_inc(S("v_ready"), 1)
            dve.wait_ge(S("rstd0_ready"), 1)
            v.tensor_scalar(rstd1[:, :], rstd0[:, :], XSCALE, None, ALU.mult).then_inc(S("rstd1_ready"), 1)
            dve.wait_ge(S("rstd1_ready"), 1)
            for t in range(T):
                last = v.tensor_scalar(xn[:, t, :], x_in[:, t, :], mean1[:, t:t + 1], rstd1[:, t:t + 1],
                                       ALU.subtract, ALU.mult)
            last.then_inc(S("xn_ready"), 1)
            dve.wait_ge(S("xn_ready"), 1)
            dve.wait_ge(S("xp_high"), 1)
            v.tensor_tensor(xp[:, :, D:2 * D], xn[:, :, :], xp[:, :, 0:D], ALU.subtract).then_inc(S("xp_ready"), 1)
            dve.wait_ge(S("const_ready"), CONSTS)

            def step(i, b, convert, aggregate, front, route):
                fi, fb = item(i, b, 2, 2)
                rb = item(i, b, 3, 2)[1]

                def convert_part(h):
                    dve.wait_ge(S("adj_loaded", f"{b}{h}"), 16 * i + 16)
                    after(dve, "agg_done", i, b, 2)
                    v.tensor_scalar(a16[b][:, h * JT * P:(h + 1) * JT * P], adj32[b][h][:, :], 1.0, None,
                                    ALU.is_equal).then_inc(S("converted", f"{b}{h}"), 1)

                if front:
                    after(dve, "agg_done", i, b, 2)
                    after(dve, "lo_ready", i, b, 4)
                    then(v.reciprocal(rdeg[fb][:, :], psA[fb][:, 2 * D:2 * D + 1]), "rdeg_ready", fb)
                if convert:
                    convert_part(0)
                if front:
                    after(dve, "lo_ready", i, b, 2)
                    after(dve, "aggT_done", i, b, 4)
                    then(v.scalar_tensor_tensor(agg[fb][:, :], psA[fb][:, 0:D], rdeg[fb][:, 0:1],
                                                lo_part[fb][:, :], ALU.mult, ALU.add), "agg_ready", fb)
                if convert:
                    convert_part(1)
                if front:
                    after(dve, "gnn_done", i, b, 2)
                    after(dve, "x1_kept", i, b, 4)
                    dve.wait_ge(S("xb_ready"), 1)
                    then(v.tensor_tensor(x1[fb][:, :], psG[:, 0:D], x_in[:, 2 * fi + fb, :], ALU.add),
                         "x1_ready", fb)
                if route:
                    after(dve, "logits_done", i, b, 3)
                    after(dve, "exp_ready", i, b, 5)
                    then(v.tensor_reduce(neg_max[rb][:, :], psG[:, 0:E], axis=AX.X, op=ALU.max, negate=True),
                         "max_ready", rb)
                if front:
                    after(dve, "x1_ready", i, b, 2)
                    then(v.bn_stats(st2[fb][:, :], x1[fb][:, :]), "st2_ready", fb)
                    after(dve, "st2_ready", i, b, 2)
                    apart(dve)
                    then(v.bn_aggr(mv2[fb][:, :], st2[fb][:, :]), "mv2_ready", fb)
                    after(dve, "mv2_ready", i, b, 2)
                    after(dve, "rstd2_ready", i, b, 4)
                    then(v.tensor_scalar(ve2[fb][:, :], mv2[fb][:, 1:2], EPS, None, ALU.add), "ve_ready", fb)
                if route:
                    after(dve, "exp_ready", i, b, 3)
                    then(v.reciprocal(rsum[:, :], exp_sum[rb][:, :]), "rsum_ready", rb)
                    after(dve, "rsum_ready", i, b, 3)
                    then(v.tensor_scalar(probs[:, :], expo[rb][:, :], rsum[:, 0:1], None, ALU.mult),
                         "probs_ready", rb)
                    after(dve, "probs_ready", i, b, 3)
                    apart(dve)
                    then(v.max(top8[:, :], probs[:, :]), "top_ready", rb)
                    after(dve, "top_ready", i, b, 3)
                    then(v.tensor_tensor(den[:, :], top8[:, 0:1], top8[:, 1:2], ALU.add), "den_ready", rb)
                    then(v.max_index(idx8[:, :], top8[:, :], probs[:, :]), "idx_ready", rb)
                    after(dve, "idx_ready", i, b, 3)
                    then(v.tensor_copy(idxf[:, :], idx8[:, 0:2]), "idxf_ready", rb)
                    after(dve, "den_ready", i, b, 3)
                    then(v.reciprocal(rden[:, :], den[:, :]), "rden_ready", rb)
                    after(dve, "idxf_ready", i, b, 3)
                    for k in two:
                        then(v.tensor_scalar(onehot[k][:, :], iota_e[:, :], idxf[:, k:k + 1], None,
                                             ALU.is_equal), "onehot_ready", rb)
                    oi = item(i, b, 3, 2)[0]
                    dve.wait_ge(S("onehot_ready"), 2 * (2 * oi + rb) + 2)
                    after(dve, "rank_done", i, b, 4)
                    then(v.tensor_tensor(mask[:, :], onehot[0][:, :], onehot[1][:, :], ALU.add), "mask_ready", rb)
                    if not (isinstance(oi, int) and oi == 0):
                        for k in two:
                            dve.wait_ge(S(f"routed_{k}", rb), 16 * oi)
                    after(dve, "rden_ready", i, b, 3)
                    for k in two:
                        then(v.tensor_scalar(row[rb][k][:, WEIGHT:WEIGHT + 1], top8[:, k:k + 1], rden[:, 0:1],
                                             0.5, ALU.mult, ALU.mult), "weight_ready", rb)
                if front:
                    after(dve, "rstd2_ready", i, b, 2)
                    if not (isinstance(fi, int) and fi == 0):
                        dve.wait_ge(S("routed_0", fb), 16 * fi)
                    then(v.tensor_scalar(row[fb][0][:, 0:D], x1[fb][:, :], mv2[fb][:, 0:1], rstd2[fb][:, 0:1],
                                         ALU.subtract, ALU.mult), "yn_ready", fb)
                if route:
                    after(dve, "rank_done", i, b, 3)
                    then(v.tensor_tensor(place[:, :], psG[:, 0:E], base_tok[:, :], ALU.add), "place_ready", rb)
                    then(v.tensor_tensor(mask_sum[:, :], mask_sum[:, :], mask[:, :], ALU.add), "mask_summed", rb)
                    after(dve, "place_ready", i, b, 3)
                    for k in two:
                        then(v.tensor_tensor_reduce(out=picked[k][:, :], in0=onehot[k][:, :], in1=place[:, :],
                                                    scale=1.0, scalar=trash[:, 0:1], op0=ALU.mult, op1=ALU.add,
                                                    accum_out=posf[:, k:k + 1]), "picked_ready", rb)
                    dve.wait_ge(S("picked_ready"), 2 * (2 * oi + rb) + 2)
                    then(v.tensor_copy(pos[rb][:, :], posf[:, :]), "pos_ready", rb)
                    after(dve, "mask_summed", i, b, 3)

            tile_pipeline(dve, step)

            dve.wait_ge(S("counts_done"), 1)
            then(v.tensor_scalar(full0[:, :], psG[0:E, 0:1], (P - 1) / 2.0, 1.0 / P, ALU.add, ALU.mult), "list_0")
            v.tensor_tensor(endf[:, :], psG[0:1, 32:32 + E], region_row[:, :], ALU.add).then_inc(S("endf_ready"), 1)
            dve.wait_ge(S("endf_ready"), 1)
            then(v.tensor_copy(endi[:, :], endf[:, :]), "ends_ready")
            dve.wait_ge(S("list_0"), 1)
            then(v.tensor_scalar(full[:, :], full0[:, :], ROUNDER, ROUNDER, ALU.add, ALU.subtract), "list_1")
            dve.wait_ge(S("list_1"), 1)
            then(v.tensor_tensor(new[:, :], full[:, :], full_prev[:, :], ALU.subtract), "new_ready")
            dve.wait_ge(S("new_ready"), 1)
            dve.wait_ge(S("seq_done"), 1)
            then(v.tensor_copy(seq[:, :], psG[0:E, 0:1]), "list_2")
            dve.wait_ge(S("list_2"), 1)
            then(v.tensor_tensor(end[:, :], seq[:, :], new[:, :], ALU.add), "list_3")
            then(v.tensor_tensor(lag[:, :], full_prev[:, :], seq[:, :], ALU.subtract), "list_3")
            then(v.tensor_scalar(since[:, :], iota_n[:, :], seq[:, 0:1], None, ALU.is_ge), "list_3")
            dve.wait_ge(S("list_3"), 3)
            then(v.tensor_scalar(off[:, :], lag[:, :], float(P), base_col[:, 0:1], ALU.mult, ALU.add), "list_4")
            then(v.scalar_tensor_tensor(holds[:, :], iota_n[:, :], end[:, 0:1], since[:, :], ALU.is_lt, ALU.mult),
                 "list_4")
            dve.wait_ge(S("list_4"), 2)
            then(v.scalar_tensor_tensor(offs[:, :], iota_n128[:, :], off[:, 0:1], holds[:, :], ALU.add, ALU.mult),
                 "offs_ready")
            dve.wait_ge(S("tab_done"), 1)
            then(v.tensor_tensor(tabf[:, :], tabf[:, :], psG[0:1, 0:2 * BLOCKS], ALU.add), "tabf_ready")
            dve.wait_ge(S("tabf_ready"), 1)
            then(v.tensor_copy(tab[:, :], tabf[:, :]), "tab_ready")

            def block_step(i, b, start, first, middle, last):
                if first:
                    fb = item(i, b, 1, 4)[1]
                    after(dve, "th_ready", i, b, 1, 4)
                    after(dve, "hid_ready", i, b, 3, 4)
                    then(v.scalar_tensor_tensor(gated[fb % 2][:, :], th[fb % 2][:, :], 1.0, psH[fb % 2][:, 0:H],
                                                ALU.add, ALU.mult), "gated_ready", fb)
                    after(dve, "gated_ready", i, b, 1, 4)
                    after(dve, "hidT_done", i, b, 3, 4)
                    then(v.tensor_tensor(hid[fb % 2][:, :], gated[fb % 2][:, :], psH[fb % 2][:, H:2 * H],
                                         ALU.mult), "hid_ready", fb)

            block_pipeline(dve, block_step)

            for c, (a, z) in enumerate(CHUNKS):
                dve.wait_ge(S("back_loaded", c), 16)
                then(v.tensor_tensor(xn[:, a:z, :], back[:, a:z, 0:D], back[:, a:z, D:2 * D], ALU.add), "added")
                dve.wait_ge(S("added"), c + 1)
                if c == 0:
                    dve.wait_ge(S("x1_kept"), T)
                then(v.tensor_tensor(xn[:, a:z, :], xn[:, a:z, :], x1_all[:, a:z, :], ALU.add), "combined")

        @block.tensor
        def _(pe):
            mm = nc.tensor.matmul

            def transpose(out_, in_):
                return nc.tensor.transpose(out_, in_, ident[:, :])

            pe.wait_ge(S("const_ready"), CONSTS)
            for name in ("wt_loaded", "gw_loaded", "gb_loaded"):
                pe.wait_ge(S(name), 16)
            pe.wait_ge(S("xp_high"), 1)
            pe.wait_ge(S("xp_ready"), 1)

            def step(i, b, convert, aggregate, front, route):
                ab = item(i, b, 1, 2)[1]
                ai = item(i, b, 1, 2)[0]
                fb = item(i, b, 2, 2)[1]
                rb = item(i, b, 3, 2)[1]

                def aggregate_part(a, z):
                    if not aggregate:
                        return
                    if a == 0:
                        after(pe, "agg_ready", i, b, 3)
                    for j in range(a, z):
                        if j % JT == 0:
                            pe.wait_ge(S("converted", f"{ab}{j // JT}"), ai + 1)
                        last = mm(psA[ab][:, 0:2 * D + 1], a16[ab][:, j * P:(j + 1) * P], xp[:, j, 0:2 * D + 1],
                                  start=(j == 0), stop=(j == T - 1))
                    if z == T:
                        last.then_inc(S("agg_done", ab), 1)

                aggregate_part(0, 7)
                if front:
                    after(pe, "agg_ready", i, b, 2)
                    after(pe, "ynT_ready", i, b, 3)
                    transpose(psT[:, 0:P], agg[fb][:, :]).then_inc(S("aggT_done", fb), 1)
                aggregate_part(7, 13)
                if front:
                    after(pe, "aggT_ready", i, b, 2)
                    after(pe, "place_ready", i, b, 4)
                    mm(psG[:, 0:D], aggT[fb][:, :], wt_s[:, :], start=True, stop=True)\
                        .then_inc(S("gnn_done", fb), 1)
                aggregate_part(13, 18)
                if route:
                    if front:
                        after(pe, "x1_ready", i, b, 2)
                    else:
                        after(pe, "place_ready", i, b, 4)
                    after(pe, "ynT_ready", i, b, 3)
                    mm(psG[:, 0:E], ynT[rb][:, :], gw_s[:, :], start=True, stop=False)
                    mm(psG[:, 0:E], onesf[0:1, :], gb_s[:, :], start=False, stop=True)\
                        .then_inc(S("logits_done", rb), 1)
                aggregate_part(18, 22)
                if front:
                    after(pe, "yn_ready", i, b, 2)
                    transpose(psT[:, 0:P], row[fb][0][:, 0:D]).then_inc(S("ynT_done", fb), 1)
                aggregate_part(22, T)
                if route:
                    after(pe, "mask_ready", i, b, 3)
                    after(pe, "mask_summed", i, b, 4)
                    mm(psG[:, 0:E], tri[:, :], mask[:, :], start=True, stop=False)
                    mm(psG[:, 0:E], ones[:, :], mask_sum[:, :], start=False, stop=True)\
                        .then_inc(S("rank_done", rb), 1)

            tile_pipeline(pe, step)

            pe.wait_ge(S("mask_summed"), T)
            pe.wait_ge(S("place_ready"), T)
            mm(psG[0:E, 0:1], mask_sum[:, :], ones[:, 0:1], start=True, stop=True)
            mm(psG[0:1, 32:32 + E], ones[:, 0:1], mask_sum[:, :], start=True, stop=True)\
                .then_inc(S("counts_done"), 1)
            pe.wait_ge(S("endf_ready"), 1)
            pe.wait_ge(S("new_ready"), 1)
            mm(psG[0:E, 0:1], tri16[:, :], new[:, :], start=True, stop=False)
            mm(psG[0:E, 0:1], onesf[0:E, 0:E], full_prev[:, :], start=False, stop=True).then_inc(S("seq_done"), 1)
            pe.wait_ge(S("list_2"), 1)
            pe.wait_ge(S("offs_ready"), 1)
            pe.wait_ge(S("list_4"), 2)
            mm(psG[0:1, 0:BLOCKS], onesf[0:E, 0:1], offs[:, :], start=True, stop=True)
            mm(psG[0:1, BLOCKS:2 * BLOCKS], e_col[:, 0:1], holds[:, :], start=True, stop=True)\
                .then_inc(S("tab_done"), 1)

            pe.wait_ge(S("tab_ready"), 1)
            pe.wait_ge(S("weights_loaded"), 16 * 3 * E)

            def block_step(i, b, start, first, middle, last):
                if start:
                    pe.wait_ge(S("block_loaded", b), 16 * i + 16)
                    after(pe, "xT_ready", i, b, 1, 4)
                    after(pe, "y_ready", i, b, 4, 4)
                    transpose(psXY[:, 0:P], xblk[b][:, 0:D]).then_inc(S("xT_done", b), 1)
                if first:
                    fi, fb = item(i, b, 1, 4)
                    e = pe.value_load(tab[0:1, bass.ds(4 * fi + fb + BLOCKS, 1)], min_val=0, max_val=E - 1)
                    after(pe, "xT_ready", i, b, 1, 4)
                    after(pe, "hid_ready", i, b, 3, 4)
                    mm(psH[fb % 2][:, :], xT[fb % 2][:, :], w12[:, bass.ds(e * (2 * H), 2 * H)], start=True,
                       stop=True).then_inc(S("h_done", fb), 1)
                if last:
                    li, lb = item(i, b, 3, 4)
                    e = pe.value_load(tab[0:1, bass.ds(4 * li + lb + BLOCKS, 1)], min_val=0, max_val=E - 1)
                    after(pe, "hidT_ready", i, b, 3, 4)
                    if start:
                        after(pe, "xT_ready", i, b, 0, 4)
                    else:
                        after(pe, "y_ready", i, b, 4, 4)
                    for c in two:
                        m = mm(psXY[:, P:2 * P], hidT[lb % 2][:, c * P:(c + 1) * P],
                               w3s[:, bass.ds(e * H + c * D, D)], start=(c == 0), stop=(c == 1))
                    m.then_inc(S("y_done", lb), 1)
                if middle:
                    mb = item(i, b, 2, 4)[1]
                    after(pe, "hid_ready", i, b, 2, 4)
                    after(pe, "hidT_ready", i, b, 3, 4)
                    for c in two:
                        m = transpose(psHT[:, c * P:(c + 1) * P], hid[mb % 2][:, c * P:(c + 1) * P])
                    m.then_inc(S("hidT_done", mb), 1)

            block_pipeline(pe, block_step)


_INPUTS = ["x", "adj", "wt", "gnn_b", "gate_w", "gate_b", "w1", "w2", "w3"]


def kernel(x, adj, L0_gnn_W, L0_gnn_b, L0_ffn_gate_w, L0_ffn_gate_b, L0_ffn_w1, L0_ffn_w2, L0_ffn_w3):
    import concourse.bacc as bacc
    from concourse.bass_utils import run_bass_kernel_spmd

    x, adj = np.asarray(x), np.asarray(adj)
    n = x.shape[0]
    T = -(-n // P)
    T += T % 2
    pad = T * P - n
    xt = np.pad(x, ((0, pad), (0, 0)), mode="edge").reshape(T, P, D).transpose(1, 0, 2).reshape(P, T * D)
    a = np.pad(np.pad(adj, ((0, pad), (0, 0)), mode="edge"), ((0, 0), (0, pad)))
    a = a.reshape(T, P, T, P).transpose(0, 3, 2, 1).reshape(T, P, T * P)
    arrays = dict(x=xt, adj=a, wt=np.asarray(L0_gnn_W).T, gnn_b=L0_gnn_b, gate_w=L0_ffn_gate_w,
                  gate_b=L0_ffn_gate_b, w1=L0_ffn_w1, w2=L0_ffn_w2, w3=L0_ffn_w3)
    arrays = {k: np.ascontiguousarray(v) for k, v in arrays.items()}
    nc = bacc.Bacc("TRN2", target_bir_lowering=False, num_devices=1)
    aps = [nc.dram_tensor(k, arrays[k].shape, mybir.dt.from_np(arrays[k].dtype), kind="ExternalInput").ap()
           for k in _INPUTS]
    out = nc.dram_tensor("out", (n, D), mybir.dt.float32, kind="ExternalOutput").ap()
    adj_ffn(nc, *aps, out)
    r = run_bass_kernel_spmd(nc, [arrays], core_ids=[0])
    return r.results[0]["out"]
```

```python
from contextlib import ExitStack

import numpy as np
import concourse.bass as bass
from concourse import mybir

P = 128
D = 128
E = 16
H = 256
EPS = 1e-5
XSCALE = 4096.0
XPW = 264
ROW = 132
DEST, WEIGHT = 128, 129
NOWHERE = 1 << 20
ROUNDER = 12582912.0
JH = 2
U = 8
WE = 3 * H


def adj_ffn(nc, x, adj, wt, gnn_b, gate_w, gate_b, w1, w2, w3, out):
    f32, f16, bf16, i32, u32 = (mybir.dt.float32, mybir.dt.float16, mybir.dt.bfloat16,
                                mybir.dt.int32, mybir.dt.uint32)
    ALU, ACT, AX = mybir.AluOpType, mybir.ActivationFunctionType, mybir.AxisListType

    T = x.shape[1] // D
    JT = T // JH
    PAIRS = T // 2
    BOUND = T * P * 2 - 1
    BLOCKS = (T * P * 2 + E * (P - 1)) // P
    BLOCKS += -BLOCKS % 4
    REGION = T * P + P
    TRASH = E * REGION
    DUMMY = TRASH + P
    ROWS = DUMMY + P
    n_tokens = out.shape[0]
    CHUNKS = [(a, min(a + 7, T)) for a in range(0, T, 7)]
    LOGITS, RANKS = 2 * D, 2 * D + 2 * E
    CONSTS = 19

    routed = nc.dram_tensor("routed_rows", [ROWS, ROW], f32).ap()
    returned = nc.dram_tensor("returned_rows", [T * P * 2, D], f32).ap()

    ctx = ExitStack()
    with ctx:
        def sb(name, shape, dt):
            return ctx.enter_context(nc.sbuf_tensor(name, shape, dt))

        def bank(name):
            return ctx.enter_context(nc.psum_tensor(name, [P, 512], f32))

        sems = {}

        BY_BUFFER = {"adj_loaded", "converted", "agg_done", "routed", "block_loaded",
                      "y_returned", "back_loaded"}

        def S(name, b=""):
            key = f"{name}{b}" if name in BY_BUFFER else name
            if key not in sems:
                sems[key] = ctx.enter_context(nc.semaphore(key))
            return sems[key]

        x_in = sb("x_in", [P, T, D], f32)
        weights = sb("weights", [P, E * WE], f32)
        wt_s = sb("wt_s", [P, D], f32)
        gw_s = sb("gw_s", [P, E], f32)
        gb_s = sb("gb_s", [1, E], f32)
        b_rows = sb("b_rows", [P, D], f32)
        ident = sb("ident", [P, P], f32)
        tri = sb("tri", [P, P], bf16)
        ones = sb("ones", [P, P], bf16)
        onesf = sb("onesf", [P, P], f32)
        tri16 = sb("tri16", [E, E], f32)
        iota_e = sb("iota_e", [P, E], f32)
        base_tok = sb("base_tok", [P, E], f32)
        trash = sb("trash", [P, 1], f32)
        exponent = sb("exponent", [P, T], f32)
        e_col = sb("e_col", [E, 1], f32)
        base_col = sb("base_col", [E, 1], f32)
        iota_n = sb("iota_n", [E, BLOCKS], f32)
        iota_n128 = sb("iota_n128", [E, BLOCKS], f32)
        region_row = sb("region_row", [1, E], f32)
        filler = sb("filler", [P, ROW], f32)
        stats = sb("stats", [P, T, 6], f32)
        m_sum = sb("m_sum", [P, T], f32)
        m_dif = sb("m_dif", [P, T], f32)
        m_dif2 = sb("m_dif2", [P, T], f32)
        v_sum = sb("v_sum", [P, T], f32)
        v_eps = sb("v_eps", [P, T], f32)
        v_all = sb("v_all", [P, T], f32)
        mean1 = sb("mean1", [P, T], f32)
        rstd0 = sb("rstd0", [P, T], f32)
        rstd1 = sb("rstd1", [P, T], f32)
        xn = sb("xn", [P, T, D], f32)
        xp = sb("xp", [P, T, XPW], f16)
        two = range(2)
        adj32 = [[sb(f"adj32_{b}{h}", [P, JT * P], i32) for h in range(JH)] for b in two]
        a16 = [sb(f"a16_{b}", [P, T * P], f16) for b in two]
        rdeg = sb("rdeg", [P, 2], f32)
        lo_part = sb("lo_part", [P, 2, D], f32)
        agg = sb("agg", [P, 2, D], f32)
        aggT = sb("aggT", [P, 2, D], f32)
        x1 = sb("x1", [P, T, D], f32)
        st2 = sb("st2", [P, 2, 6], f32)
        mv2 = sb("mv2", [P, 2, 2], f32)
        ve2 = sb("ve2", [P, 2], f32)
        rstd2 = sb("rstd2", [P, 2], f32)
        yn = sb("yn", [P, 2, D], f32)
        ynT = sb("ynT", [P, 2, D], f32)
        row = sb("row", [P, 2, 2, ROW], f32)
        neg_max = sb("neg_max", [P, 2], f32)
        shifted = sb("shifted", [P, 2, E], f32)
        expo = sb("expo", [P, 2, E], f32)
        exp_sum = sb("exp_sum", [P, 2], f32)
        rsum = sb("rsum", [P, 2], f32)
        valid = sb("valid", [P, 2], f32)
        probs = sb("probs", [P, 2, E], f32)
        top8 = sb("top8", [P, 2, 8], f32)
        idx8 = sb("idx8", [P, 2, 8], u32)
        choice = sb("choice", [P, 2, 2], f32)
        den = sb("den", [P, 2], f32)
        rden = sb("rden", [P, 2], f32)
        onehot = sb("onehot", [P, 2, 2, E], f32)
        mask = sb("mask", [P, 2, E], bf16)
        mask_sum = sb("mask_sum", [P, E], bf16)
        place = sb("place", [P, 2, E], f32)
        picked = sb("picked", [P, 2, 2, E], f32)
        posf = sb("posf", [P, 4], f32)
        pos = sb("pos", [P, 4], i32)
        full0 = sb("full0", [E, 1], f32)
        full = sb("full", [E, 1], f32)
        full_prev = sb("full_prev", [E, 1], f32)
        new = sb("new", [E, 1], f32)
        seq = sb("seq", [E, 1], f32)
        end = sb("end", [E, 1], f32)
        lag = sb("lag", [E, 1], f32)
        off = sb("off", [E, 1], f32)
        past = sb("past", [E, BLOCKS], f32)
        holds = sb("holds", [E, BLOCKS], f32)
        offs = sb("offs", [E, BLOCKS], f32)
        tabf = sb("tabf", [1, 2 * BLOCKS], f32)
        tab = sb("tab", [1, 2 * BLOCKS], i32)
        endf = sb("endf", [1, E], f32)
        endi = sb("endi", [1, E], i32)
        four, turn = range(4), range(U)
        xblk = [sb(f"xblk{b}", [P, ROW], f32) for b in turn]
        ticket = [sb(f"ticket{b}", [P, 2], f32) for b in turn]
        xT = [sb(f"xT{b}", [P, P], f32) for b in two]
        th = [sb(f"th{b}", [P, H], f32) for b in two]
        gated = [sb(f"gated{b}", [P, H], f32) for b in two]
        hid = [sb(f"hid{b}", [P, H], f32) for b in two]
        hidT = [sb(f"hidT{b}", [P, H], f32) for b in two]
        yblk = [sb(f"yblk{b}", [P, D], f32) for b in turn]
        back = sb("back", [P, T, 2 * D], f32)

        psA = [bank(f"psA{b}") for b in two]
        psH = [bank(f"psH{b}") for b in two]
        psHT = bank("psHT")
        psXY = bank("psXY")
        psT = bank("psT")
        psG = bank("psG")
        ps_xT, ps_h, ps_hT, ps_y = [psT, psG], psH, [psHT, psA[0]], [psXY, psA[1]]

        block = ctx.enter_context(nc.Block())


        def item(i, b, back):
            return (i, b - back) if b >= back else item(i - 1, b + U, back)

        def after(eng, name, i, b, back=0):
            i, b = item(i, b, back)
            if not (isinstance(i, int) and i < 0):
                eng.wait_ge(S(name, b), i + 1 if name in BY_BUFFER else U * i + b + 1)

        def since(eng, name, s, back, b=""):
            if not (isinstance(s, int) and s < back):
                eng.wait_ge(S(name, b), s - back + 1)

        def apart(eng):
            eng.nop(nofuse=True)

        def tile_pipeline(eng, step):
            def run(s):
                on = [True] * 4 if not isinstance(s, int) else [0 <= s - back < PAIRS for back in range(4)]
                step(s, *on)
            for s in range(4):
                run(s)
            with eng.Fori(4, PAIRS) as s:
                run(s)
            for s in range(PAIRS, PAIRS + 3):
                run(s)

        def block_pipeline(eng, step):
            def run(i, b):
                s = U * i + b if isinstance(i, int) else None
                on = [s is None or 0 <= s - back < BLOCKS for back in range(5)]
                step(i, b, *on)
            for b in turn:
                run(0, b)
            with eng.Fori(1, BLOCKS // U) as i:
                for b in turn:
                    run(i, b)
            for s in range(BLOCKS // U * U, BLOCKS + 4):
                run(s // U, s % U)

        @block.sync
        def _(sp):
            sp.dma_start(x_in[:, :, :], x.rearrange("p (t d) -> p t d", d=D)).then_inc(S("x_loaded"), 16)
            sp.dma_start(b_rows[:, :], gnn_b.partition_broadcast(P)).then_inc(S("b_loaded"), 16)
            sp.dma_start(wt_s[:, :], wt).then_inc(S("wt_loaded"), 16)
            sp.dma_start(gw_s[:, :], gate_w).then_inc(S("gw_loaded"), 16)
            sp.dma_start(gb_s[:, :], gate_b.rearrange("(a e) -> a e", a=1)).then_inc(S("gb_loaded"), 16)

            def load_adjacency(i):
                for b in two:
                    for h in range(JH):
                        if not isinstance(i, int):
                            sp.wait_ge(S("converted", f"{b}{h}"), i)
                        sp.dma_start(adj32[b][h][:, :], adj[2 * i + b, :, h * JT * P:(h + 1) * JT * P])\
                            .then_inc(S("adj_loaded", f"{b}{h}"), 16)

            load_adjacency(0)
            with sp.Fori(1, PAIRS) as i:
                load_adjacency(i)
            sp.wait_ge(S("tab_ready"), 1)
            sp.wait_ge(S("tails_filled"), 16 * E)
            sp.wait_ge(S("dummy_filled"), 16)
            for n in range(4):
                sp.wait_ge(S("routed", n), 16 * PAIRS)

            def load_blocks(i, buffers=turn):
                for b in buffers:
                    first = sp.value_load(tab[0:1, bass.ds(U * i + b, 1)], min_val=0, max_val=DUMMY)
                    after(sp, "xT_done", i, b, U)
                    after(sp, "ticket_ready", i, b, U)
                    sp.dma_start(xblk[b][:, :], routed[bass.ds(first, P), :]).then_inc(S("block_loaded", b), 16)

            load_blocks(0)
            with sp.Fori(1, BLOCKS // U) as i:
                load_blocks(i)
            load_blocks(BLOCKS // U, range(BLOCKS % U))
            for b in turn:
                sp.wait_ge(S("y_returned", b), 16 * len(range(b, BLOCKS, U)))
            pairs = returned.rearrange("(t p k) d -> p t (k d)", p=P, k=2)
            for c, (a, z) in enumerate(CHUNKS):
                sp.dma_start(back[:, a:z, :], pairs[:, a:z, :]).then_inc(S("back_loaded", c), 16)
            whole = n_tokens // P
            for c, (a, z) in enumerate(CHUNKS):
                sp.wait_ge(S("combined"), c + 1)
                z = min(z, whole)
                sp.dma_start(out[a * P:z * P, :].rearrange("(t p) d -> p t d", p=P), xn[:, a:z, :])\
                    .then_inc(S("out_stored"), 16)
            left = n_tokens - whole * P
            sp.dma_start(out[whole * P:n_tokens, :], xn[0:left, whole, :]).then_inc(S("out_stored"), 16)
            sp.wait_ge(S("out_stored"), 16 * (len(CHUNKS) + 1))

        @block.scalar
        def _(act):
            act.wait_ge(S("xn_ready"), 1)
            nc.scalar.activation(xp[:, :, 0:D], xn[:, :, :], ACT.Copy).then_inc(S("xp_high"), 1)
            for e in range(E):
                o = e * WE
                act.dma_start(weights[:, o:o + H], w1[e]).then_inc(S("weights_loaded"), 16)
                act.dma_start(weights[:, o + H:o + 2 * H], w2[e]).then_inc(S("weights_loaded"), 16)
                act.dma_start(weights[:, o + 2 * H:o + WE].rearrange("p (c n) -> p c n", c=2),
                              w3[e].rearrange("(c p) n -> p c n", p=P)).then_inc(S("weights_loaded"), 16)

            def step(s, convert, aggregate, front, route):
                if front:
                    since(act, "rdeg_ready", s, 2)
                    since(act, "agg_ready", s, 3)
                    for b in two:
                        last = nc.scalar.activation(lo_part[:, b, :], psA[b][:, D:2 * D], ACT.Copy,
                                                    scale=rdeg[:, b:b + 1])
                    last.then_inc(S("lo_ready"), 1)
                if route:
                    since(act, "shift_ready", s, 3)
                    since(act, "probs_ready", s, 4)
                    nc.scalar.activation(expo[:, :, :], shifted[:, :, :], ACT.Exp).then_inc(S("exp_ready"), 1)
                if front:
                    since(act, "aggT_done", s, 2)
                    since(act, "gnn_done", s, 3)
                    nc.scalar.activation(aggT[:, :, :], psT[:, 0:2 * D].rearrange("p (b d) -> p b d", b=2),
                                         ACT.Copy).then_inc(S("aggT_ready"), 1)
                if route:
                    since(act, "yn_ready", s, 3)
                    if not (isinstance(s, int) and s == 3):
                        for n in range(4):
                            act.wait_ge(S("routed", n), 16 * (s - 3))
                    for k in two:
                        last = nc.scalar.activation(row[:, :, k, 0:D], yn[:, :, :], ACT.Copy)
                    last.then_inc(S("rows_ready"), 1)
                if front:
                    since(act, "ynT_done", s, 2)
                    since(act, "logits_done", s, 3)
                    nc.scalar.activation(ynT[:, :, :], psT[:, 0:2 * D].rearrange("p (b d) -> p b d", b=2),
                                         ACT.Copy).then_inc(S("ynT_ready"), 1)

            tile_pipeline(act, step)

            act.wait_ge(S("ends_ready"), 1)
            act.wait_ge(S("filler_ready"), 1)
            for e in range(E):
                first = act.value_load(endi[0:1, e:e + 1], min_val=0, max_val=TRASH - P)
                act.dma_start(routed[bass.ds(first, P), :], filler[:, :]).then_inc(S("tails_filled"), 16)

            def block_step(i, b, start, first, ticketing, middle, last):
                if start:
                    after(act, "xT_done", i, b, 0)
                    after(act, "h_done", i, b, 2)
                    nc.scalar.activation(xT[b % 2][:, :], ps_xT[b % 2][:, 0:P], ACT.Copy).then_inc(S("xT_ready"), 1)
                if first:
                    fb = item(i, b, 1)[1]
                    after(act, "h_done", i, b, 1)
                    after(act, "hid_ready", i, b, 3)
                    nc.scalar.activation(th[fb % 2][:, :], ps_h[fb % 2][:, 0:H], ACT.Tanh, scale=0.5)\
                        .then_inc(S("th_ready"), 1)
                if middle:
                    mb = item(i, b, 3)[1]
                    after(act, "hidT_done", i, b, 3)
                    after(act, "y_done", i, b, 5)
                    nc.scalar.activation(hidT[mb % 2][:, :], ps_hT[mb % 2][:, 0:H], ACT.Copy)\
                        .then_inc(S("hidT_ready"), 1)
                if last:
                    lb = item(i, b, 4)[1]
                    after(act, "y_done", i, b, 4)
                    after(act, "ticket_ready", i, b, 4)
                    nc.scalar.activation(yblk[lb][:, :], ps_y[lb % 2][:, 0:D], ACT.Copy,
                                         scale=ticket[lb][:, 1:2]).then_inc(S("y_ready"), 1)

            block_pipeline(act, block_step)

        @block.gpsimd
        def _(pool):
            g = nc.gpsimd
            big = dict(allow_small_or_imprecise_dtypes=True)
            g.memset(exponent[:, :], -0.5).then_inc(S("exponent_ready"), 1)
            g.memset(ident[:, :], 0.0).then_inc(S("const_memset"), 1)
            g.memset(tri[:, :], 1.0).then_inc(S("const_memset"), 1)
            g.memset(tri16[:, :], 1.0).then_inc(S("const_memset"), 1)
            g.memset(filler[:, :], 0.0).then_inc(S("const_memset"), 1)
            g.memset(row[:, :, :, :], 0.0).then_inc(S("const_memset"), 1)
            pool.wait_ge(S("const_memset"), 5)
            g.affine_select(out=ident[:, :], in_=ident[:, :], compare_op=ALU.not_equal, fill=1.0, base=0,
                            pattern=[[-1, P]], channel_multiplier=1).then_inc(S("const_ready"), 1)
            for m, n in ((tri, P), (tri16, E)):
                g.affine_select(out=m[:, :], in_=m[:, :], compare_op=ALU.is_gt, fill=0.0, base=0,
                                pattern=[[1, n]], channel_multiplier=-1).then_inc(S("const_ready"), 1)
            g.memset(filler[:, DEST:DEST + 1].bitcast(i32), NOWHERE).then_inc(S("filler_ready"), 1)
            g.iota(row[:, :, :, DEST].bitcast(i32), pattern=[[2 * P, 2], [1, 2]], base=0, channel_multiplier=2)\
                .then_inc(S("const_ready"), 1)
            g.memset(ones[:, :], 1.0).then_inc(S("const_ready"), 1)
            g.memset(onesf[:, :], 1.0).then_inc(S("const_ready"), 1)
            g.memset(mask_sum[:, :], 0.0).then_inc(S("const_ready"), 1)
            g.memset(full_prev[:, :], 0.0).then_inc(S("const_ready"), 1)
            g.memset(tabf[:, 0:BLOCKS], float(DUMMY)).then_inc(S("const_ready"), 1)
            g.memset(tabf[:, BLOCKS:2 * BLOCKS], 0.0).then_inc(S("const_ready"), 1)
            g.memset(xp[:, :, 2 * D:2 * D + 1], XSCALE).then_inc(S("const_ready"), 1)
            g.iota(iota_e[:, :], pattern=[[1, E]], base=1, channel_multiplier=0, **big).then_inc(S("const_ready"), 1)
            g.iota(base_tok[:, :], pattern=[[REGION, E]], base=-TRASH, channel_multiplier=-1, **big)\
                .then_inc(S("const_ready"), 1)
            g.iota(trash[:, :], pattern=[[0, 1]], base=TRASH, channel_multiplier=1, **big)\
                .then_inc(S("const_ready"), 1)
            g.iota(e_col[:, :], pattern=[[0, 1]], base=0, channel_multiplier=WE, **big)\
                .then_inc(S("const_ready"), 1)
            g.iota(base_col[:, :], pattern=[[0, 1]], base=-DUMMY, channel_multiplier=REGION, **big)\
                .then_inc(S("const_ready"), 1)
            g.iota(iota_n[:, :], pattern=[[1, BLOCKS]], base=0, channel_multiplier=0, **big)\
                .then_inc(S("const_ready"), 1)
            g.iota(iota_n128[:, :], pattern=[[P, BLOCKS]], base=0, channel_multiplier=0, **big)\
                .then_inc(S("const_ready"), 1)
            g.iota(region_row[:, :], pattern=[[REGION, E]], base=0, channel_multiplier=0, **big)\
                .then_inc(S("const_ready"), 1)
            pool.wait_ge(S("filler_ready"), 1)
            pool.dma_start(routed[DUMMY:DUMMY + P, :], filler[:, :]).then_inc(S("dummy_filled"), 16)
            pool.wait_ge(S("v_ready"), 1)
            pool.wait_ge(S("exponent_ready"), 1)
            g.tensor_tensor(rstd0[:, :], v_all[:, :], exponent[:, :], ALU.pow).then_inc(S("rstd0_ready"), 1)
            pool.wait_ge(S("xn_ready"), 1)
            pool.wait_ge(S("b_loaded"), 16)
            g.tensor_tensor(x_in[:, :, :], x_in[:, :, :], b_rows[:, None, :].broadcast_to([P, T, D]), ALU.add)\
                .then_inc(S("xb_ready"), 1)

            def step(s, convert, aggregate, front, route):
                first = isinstance(s, int) and s == 3
                if route and not first:
                    for n in range(4):
                        pool.wait_ge(S("routed", n), 16 * (s - 3))
                    apart(pool)
                    dest = row[:, :, :, DEST].bitcast(i32)
                    g.tensor_scalar(dest, dest, 4.0 * P, None, ALU.add).then_inc(S("dest_ready"), 1)
                if front:
                    since(pool, "ve_ready", s, 2)
                    since(pool, "yn_ready", s, 3)
                    g.tensor_tensor(rstd2[:, :], ve2[:, :], exponent[:, 0:2], ALU.pow)\
                        .then_inc(S("rstd2_ready"), 1)
                if route:
                    since(pool, "pos_ready", s, 3)
                    since(pool, "weight_ready", s, 3)
                    since(pool, "rows_ready", s, 3)
                    if not first:
                        pool.wait_ge(S("dest_ready"), s - 3)
                    apart(pool)
                    for n in range(4):
                        g.indirect_dma_start(routed[:, :], bass.IndirectOffsetOnAxis(pos[:, n:n + 1], 0),
                                             row[:, n // 2, n % 2, :], None).then_inc(S("routed", n), 16)

            pool.wait_ge(S("const_ready"), CONSTS)
            tile_pipeline(pool, step)

            def block_step(i, b, start, first, ticketing, middle, last):
                if ticketing:
                    ti, tb = item(i, b, 2)
                    pool.wait_ge(S("block_loaded", tb), 16 * ti + 16)
                    if not (isinstance(ti, int) and ti == 0):
                        pool.wait_ge(S("y_returned", tb), 16 * ti)
                    apart(pool)
                    g.tensor_copy(ticket[tb][:, :], xblk[tb][:, DEST:DEST + 2]).then_inc(S("ticket_ready"), 1)
                if last:
                    lb = item(i, b, 4)[1]
                    after(pool, "ticket_ready", i, b, 4)
                    after(pool, "y_ready", i, b, 4)
                    apart(pool)
                    g.indirect_dma_start(returned[:, :],
                                         bass.IndirectOffsetOnAxis(ticket[lb][:, 0:1].bitcast(i32), 0),
                                         yblk[lb][:, :], None, bounds_check=BOUND, oob_is_err=False)\
                        .then_inc(S("y_returned", lb), 16)

            block_pipeline(pool, block_step)

        @block.vector
        def _(dve):
            v = nc.vector

            def then(ins, name, b=""):
                ins.then_inc(S(name, b), 1)

            dve.wait_ge(S("x_loaded"), 16)
            for t in range(T):
                last = v.bn_stats(stats[:, t, :], x_in[:, t, :])
            last.then_inc(S("stats_ready"), 1)
            dve.wait_ge(S("stats_ready"), 1)
            v.tensor_tensor(m_sum[:, :], stats[:, :, 1], stats[:, :, 4], ALU.add).then_inc(S("m_ready"), 1)
            v.tensor_tensor(m_dif[:, :], stats[:, :, 1], stats[:, :, 4], ALU.subtract).then_inc(S("m_ready"), 1)
            v.tensor_tensor(v_sum[:, :], stats[:, :, 2], stats[:, :, 5], ALU.add).then_inc(S("m_ready"), 1)
            dve.wait_ge(S("m_ready"), 3)
            v.tensor_scalar(mean1[:, :], m_sum[:, :], 0.5, None, ALU.mult).then_inc(S("m2_ready"), 1)
            v.tensor_tensor(m_dif2[:, :], m_dif[:, :], m_dif[:, :], ALU.mult).then_inc(S("m2_ready"), 1)
            v.tensor_scalar(v_eps[:, :], v_sum[:, :], 1.0 / D, EPS, ALU.mult, ALU.add).then_inc(S("m2_ready"), 1)
            dve.wait_ge(S("m2_ready"), 3)
            v.scalar_tensor_tensor(v_all[:, :], m_dif2[:, :], 0.25, v_eps[:, :], ALU.mult, ALU.add)\
                .then_inc(S("v_ready"), 1)
            dve.wait_ge(S("rstd0_ready"), 1)
            v.tensor_scalar(rstd1[:, :], rstd0[:, :], XSCALE, None, ALU.mult).then_inc(S("rstd1_ready"), 1)
            dve.wait_ge(S("rstd1_ready"), 1)
            for t in range(T):
                last = v.tensor_scalar(xn[:, t, :], x_in[:, t, :], mean1[:, t:t + 1], rstd1[:, t:t + 1],
                                       ALU.subtract, ALU.mult)
            last.then_inc(S("xn_ready"), 1)
            dve.wait_ge(S("xn_ready"), 1)
            dve.wait_ge(S("xp_high"), 1)
            v.tensor_tensor(xp[:, :, D:2 * D], xn[:, :, :], xp[:, :, 0:D], ALU.subtract).then_inc(S("xp_ready"), 1)
            dve.wait_ge(S("const_ready"), CONSTS)

            def step(s, convert, aggregate, front, route):
                def convert_part(b, h):
                    dve.wait_ge(S("adj_loaded", f"{b}{h}"), 16 * s + 16)
                    since(dve, "agg_done", s, 1, b)
                    v.tensor_scalar(a16[b][:, h * JT * P:(h + 1) * JT * P], adj32[b][h][:, :], 1.0, None,
                                    ALU.is_equal).then_inc(S("converted", f"{b}{h}"), 1)

                def spread(ap):
                    return ap[:, :, None].broadcast_to([P, 2, E])

                if front:
                    since(dve, "agg_done", s, 2, 0)
                    since(dve, "agg_done", s, 2, 1)
                    since(dve, "agg_ready", s, 3)
                    for b in two:
                        last = v.reciprocal(rdeg[:, b:b + 1], psA[b][:, 2 * D:2 * D + 1])
                    then(last, "rdeg_ready")
                if route:
                    since(dve, "logits_done", s, 3)
                    logits = psG[:, LOGITS:LOGITS + 2 * E].rearrange("p (b e) -> p b e", b=2)
                    then(v.tensor_reduce(neg_max[:, :], logits, axis=AX.X, op=ALU.max, negate=True), "max_ready")
                    since(dve, "max_ready", s, 3)
                    since(dve, "exp_ready", s, 4)
                    then(v.tensor_tensor(shifted[:, :, :], logits, spread(neg_max), ALU.add), "shift_ready")
                if front:
                    since(dve, "lo_ready", s, 2)
                    since(dve, "aggT_done", s, 3)
                    for b in two:
                        last = v.scalar_tensor_tensor(agg[:, b, :], psA[b][:, 0:D], rdeg[:, b:b + 1],
                                                      lo_part[:, b, :], ALU.mult, ALU.add)
                    then(last, "agg_ready")
                if route:
                    since(dve, "exp_ready", s, 3)
                    then(v.tensor_reduce(exp_sum[:, :], expo[:, :, :], axis=AX.X, op=ALU.add), "sum_ready")
                    since(dve, "sum_ready", s, 3)
                    then(v.reciprocal(rsum[:, :], exp_sum[:, :]), "rsum_ready")
                    v.tensor_scalar(valid[:, :], exp_sum[:, :], 0.5, None, ALU.is_ge).then_inc(S("valid_ready"), 1)
                    since(dve, "rsum_ready", s, 3)
                    then(v.tensor_tensor(probs[:, :, :], expo[:, :, :], spread(rsum), ALU.mult), "probs_ready")
                    since(dve, "probs_ready", s, 3)
                    apart(dve)
                    for b in two:
                        last = v.max(top8[:, b, :], probs[:, b, :])
                    then(last, "top_ready")
                    since(dve, "top_ready", s, 3)
                    then(v.tensor_tensor(den[:, :], top8[:, :, 0], top8[:, :, 1], ALU.add), "den_ready")
                    for b in two:
                        last = v.max_index(idx8[:, b, :], top8[:, b, :], probs[:, b, :])
                    then(last, "idx_ready")
                    since(dve, "den_ready", s, 3)
                    then(v.reciprocal(rden[:, :], den[:, :]), "rden_ready")
                    since(dve, "idx_ready", s, 3)
                    since(dve, "valid_ready", s, 3)
                    then(v.scalar_tensor_tensor(choice[:, :, :], idx8[:, :, 0:2], 1.0,
                                                valid[:, :, None].broadcast_to([P, 2, 2]), ALU.add, ALU.mult),
                         "choice_ready")
                    since(dve, "choice_ready", s, 3)
                    then(v.tensor_tensor(onehot[:, :, :, :],
                                         iota_e[:, None, None, :].broadcast_to([P, 2, 2, E]),
                                         choice[:, :, :, None].broadcast_to([P, 2, 2, E]), ALU.is_equal),
                         "onehot_ready")
                    since(dve, "onehot_ready", s, 3)
                    since(dve, "rank_done", s, 4)
                    since(dve, "mask_summed", s, 4)
                    then(v.tensor_tensor(mask[:, :, :], onehot[:, :, 0, :], onehot[:, :, 1, :], ALU.add),
                         "mask_ready")
                    since(dve, "rden_ready", s, 3)
                    if not (isinstance(s, int) and s == 3):
                        for n in range(4):
                            dve.wait_ge(S("routed", n), 16 * (s - 3))
                    then(v.scalar_tensor_tensor(row[:, :, :, WEIGHT], top8[:, :, 0:2], 0.5,
                                                rden[:, :, None].broadcast_to([P, 2, 2]), ALU.mult, ALU.mult),
                         "weight_ready")
                if front:
                    f = s - 2
                    since(dve, "gnn_done", s, 2)
                    if isinstance(s, int) and s == 2:
                        dve.wait_ge(S("xb_ready"), 1)
                    pair = slice(2 * f, 2 * f + 2) if isinstance(f, int) else bass.ds(2 * f, 2)
                    then(v.tensor_tensor(x1[:, pair, :], psG[:, 0:2 * D].rearrange("p (b d) -> p b d", b=2),
                                         x_in[:, pair, :], ALU.add), "x1_ready")
                    since(dve, "x1_ready", s, 2)
                    apart(dve)
                    for b in two:
                        last = v.bn_stats(st2[:, b, :], x1[:, 2 * f + b, :])
                    then(last, "st2_ready")
                    since(dve, "st2_ready", s, 2)
                    apart(dve)
                    for b in two:
                        last = v.bn_aggr(mv2[:, b, :], st2[:, b, :])
                    then(last, "mv2_ready")
                    since(dve, "mv2_ready", s, 2)
                    since(dve, "rstd2_ready", s, 3)
                    then(v.tensor_scalar(ve2[:, :], mv2[:, :, 1], EPS, None, ALU.add), "ve_ready")
                if route:
                    since(dve, "rank_done", s, 3)
                    then(v.tensor_tensor(place[:, :, :], psG[:, RANKS:RANKS + 2 * E]
                                         .rearrange("p (b e) -> p b e", b=2),
                                         base_tok[:, None, :].broadcast_to([P, 2, E]), ALU.add), "place_ready")
                    then(v.tensor_tensor(mask_sum[:, :], mask_sum[:, :], mask[:, 0, :], ALU.add), "mask_summed_0")
                    since(dve, "place_ready", s, 3)
                    then(v.tensor_tensor(picked[:, :, :, :], onehot[:, :, :, :],
                                         place[:, :, None, :].broadcast_to([P, 2, 2, E]), ALU.mult),
                         "picked_ready")
                    since(dve, "mask_summed_0", s, 3)
                    then(v.tensor_tensor(mask_sum[:, :], mask_sum[:, :], mask[:, 1, :], ALU.add), "mask_summed")
                    since(dve, "picked_ready", s, 3)
                    then(v.tensor_reduce(posf[:, :], picked[:, :, :, :].rearrange("p b k e -> p (b k) e"),
                                         axis=AX.X, op=ALU.add), "posf_ready")
                    since(dve, "posf_ready", s, 3)
                    then(v.tensor_scalar(pos[:, :], posf[:, :], trash[:, 0:1], None, ALU.add), "pos_ready")
                if convert:
                    convert_part(0, 0)
                    convert_part(0, 1)
                if front:
                    since(dve, "rstd2_ready", s, 2)
                    since(dve, "rows_ready", s, 3)
                    since(dve, "ynT_done", s, 3)
                    for b in two:
                        last = v.tensor_scalar(yn[:, b, :], x1[:, 2 * f + b, :], mv2[:, b, 0:1], rstd2[:, b:b + 1],
                                               ALU.subtract, ALU.mult)
                    then(last, "yn_ready")
                if convert:
                    convert_part(1, 0)
                    convert_part(1, 1)

            tile_pipeline(dve, step)

            dve.wait_ge(S("counts_done"), 1)
            then(v.tensor_scalar(full0[:, :], psG[0:E, 0:1], (P - 1) / 2.0, 1.0 / P, ALU.add, ALU.mult), "list_0")
            v.tensor_tensor(endf[:, :], psG[0:1, 32:32 + E], region_row[:, :], ALU.add).then_inc(S("endf_ready"), 1)
            dve.wait_ge(S("endf_ready"), 1)
            then(v.tensor_copy(endi[:, :], endf[:, :]), "ends_ready")
            dve.wait_ge(S("list_0"), 1)
            then(v.tensor_scalar(full[:, :], full0[:, :], ROUNDER, ROUNDER, ALU.add, ALU.subtract), "list_1")
            dve.wait_ge(S("list_1"), 1)
            then(v.tensor_tensor(new[:, :], full[:, :], full_prev[:, :], ALU.subtract), "new_ready")
            dve.wait_ge(S("new_ready"), 1)
            dve.wait_ge(S("seq_done"), 1)
            then(v.tensor_copy(seq[:, :], psG[0:E, 0:1]), "list_2")
            dve.wait_ge(S("list_2"), 1)
            then(v.tensor_tensor(end[:, :], seq[:, :], new[:, :], ALU.add), "list_3")
            then(v.tensor_tensor(lag[:, :], full_prev[:, :], seq[:, :], ALU.subtract), "list_3")
            then(v.tensor_scalar(past[:, :], iota_n[:, :], seq[:, 0:1], None, ALU.is_ge), "list_3")
            dve.wait_ge(S("list_3"), 3)
            then(v.tensor_scalar(off[:, :], lag[:, :], float(P), base_col[:, 0:1], ALU.mult, ALU.add), "list_4")
            then(v.scalar_tensor_tensor(holds[:, :], iota_n[:, :], end[:, 0:1], past[:, :], ALU.is_lt, ALU.mult),
                 "list_4")
            dve.wait_ge(S("list_4"), 2)
            then(v.scalar_tensor_tensor(offs[:, :], iota_n128[:, :], off[:, 0:1], holds[:, :], ALU.add, ALU.mult),
                 "offs_ready")
            dve.wait_ge(S("tab_done"), 1)
            then(v.tensor_tensor(tabf[:, :], tabf[:, :], psG[0:1, 0:2 * BLOCKS], ALU.add), "tabf_ready")
            dve.wait_ge(S("tabf_ready"), 1)
            then(v.tensor_copy(tab[:, :], tabf[:, :]), "tab_ready")

            def block_step(i, b, start, first, ticketing, middle, last):
                if first:
                    fb = item(i, b, 1)[1]
                    after(dve, "th_ready", i, b, 1)
                    after(dve, "hid_ready", i, b, 3)
                    then(v.scalar_tensor_tensor(gated[fb % 2][:, :], th[fb % 2][:, :], 1.0, ps_h[fb % 2][:, 0:H],
                                                ALU.add, ALU.mult), "gated_ready", fb)
                    after(dve, "gated_ready", i, b, 1)
                    after(dve, "hidT_done", i, b, 3)
                    then(v.tensor_tensor(hid[fb % 2][:, :], gated[fb % 2][:, :], ps_h[fb % 2][:, H:2 * H],
                                         ALU.mult), "hid_ready", fb)

            block_pipeline(dve, block_step)

            for c, (a, z) in enumerate(CHUNKS):
                dve.wait_ge(S("back_loaded", c), 16)
                then(v.tensor_tensor(xn[:, a:z, :], back[:, a:z, 0:D], back[:, a:z, D:2 * D], ALU.add), "added")
                dve.wait_ge(S("added"), c + 1)
                then(v.tensor_tensor(xn[:, a:z, :], xn[:, a:z, :], x1[:, a:z, :], ALU.add), "combined")

        @block.tensor
        def _(pe):
            mm = nc.tensor.matmul

            def transpose(out_, in_):
                return nc.tensor.transpose(out_, in_, ident[:, :])

            pe.wait_ge(S("const_ready"), CONSTS)
            for name in ("wt_loaded", "gw_loaded", "gb_loaded"):
                pe.wait_ge(S(name), 16)
            pe.wait_ge(S("xp_high"), 1)
            pe.wait_ge(S("xp_ready"), 1)

            def step(s, convert, aggregate, front, route):
                def aggregate_part(b, a, z):
                    if not aggregate:
                        return
                    if a == 0:
                        since(pe, "agg_ready", s, 2)
                    for j in range(a, z):
                        if j % JT == 0:
                            pe.wait_ge(S("converted", f"{b}{j // JT}"), s)
                        last = mm(psA[b][:, 0:2 * D + 1], a16[b][:, j * P:(j + 1) * P], xp[:, j, 0:2 * D + 1],
                                  start=(j == 0), stop=(j == T - 1))
                    if z == T:
                        last.then_inc(S("agg_done", b), 1)

                if route:
                    since(pe, "ynT_ready", s, 3)
                    since(pe, "place_ready", s, 4)
                    for b in two:
                        o = psG[:, LOGITS + b * E:LOGITS + (b + 1) * E]
                        mm(o, ynT[:, b, :], gw_s[:, :], start=True, stop=False)
                        last = mm(o, onesf[0:1, :], gb_s[:, :], start=False, stop=True)
                    last.then_inc(S("logits_done"), 1)
                aggregate_part(0, 0, 9)
                if front:
                    since(pe, "agg_ready", s, 2)
                    since(pe, "ynT_ready", s, 3)
                    for b in two:
                        last = transpose(psT[:, b * D:(b + 1) * D], agg[:, b, :])
                    last.then_inc(S("aggT_done"), 1)
                aggregate_part(0, 9, 18)
                if front:
                    since(pe, "aggT_ready", s, 2)
                    if route:
                        since(pe, "shift_ready", s, 3)
                    for b in two:
                        last = mm(psG[:, b * D:(b + 1) * D], aggT[:, b, :], wt_s[:, :], start=True, stop=True)
                    last.then_inc(S("gnn_done"), 1)
                aggregate_part(0, 18, 23)
                if route:
                    since(pe, "mask_ready", s, 3)
                    since(pe, "mask_summed", s, 4)
                    if front:
                        since(pe, "x1_ready", s, 2)
                    for b in two:
                        o = psG[:, RANKS + b * E:RANKS + (b + 1) * E]
                        mm(o, tri[:, :], mask[:, b, :], start=True, stop=False)
                        last = mm(o, ones[:, :], mask_sum[:, :], start=False, stop=(b == 0))
                    mm(o, ones[:, :], mask[:, 0, :], start=False, stop=True).then_inc(S("rank_done"), 1)
                aggregate_part(0, 23, T)
                aggregate_part(1, 0, T)
                if front:
                    since(pe, "yn_ready", s, 2)
                    for b in two:
                        last = transpose(psT[:, b * D:(b + 1) * D], yn[:, b, :])
                    last.then_inc(S("ynT_done"), 1)

            tile_pipeline(pe, step)

            pe.wait_ge(S("mask_summed"), PAIRS)
            pe.wait_ge(S("place_ready"), PAIRS)
            mm(psG[0:E, 0:1], mask_sum[:, :], ones[:, 0:1], start=True, stop=True)
            mm(psG[0:1, 32:32 + E], ones[:, 0:1], mask_sum[:, :], start=True, stop=True)\
                .then_inc(S("counts_done"), 1)
            pe.wait_ge(S("endf_ready"), 1)
            pe.wait_ge(S("new_ready"), 1)
            mm(psG[0:E, 0:1], tri16[:, :], new[:, :], start=True, stop=False)
            mm(psG[0:E, 0:1], onesf[0:E, 0:E], full_prev[:, :], start=False, stop=True).then_inc(S("seq_done"), 1)
            pe.wait_ge(S("list_2"), 1)
            pe.wait_ge(S("offs_ready"), 1)
            pe.wait_ge(S("list_4"), 2)
            mm(psG[0:1, 0:BLOCKS], onesf[0:E, 0:1], offs[:, :], start=True, stop=True)
            mm(psG[0:1, BLOCKS:2 * BLOCKS], e_col[:, 0:1], holds[:, :], start=True, stop=True)\
                .then_inc(S("tab_done"), 1)

            pe.wait_ge(S("tab_ready"), 1)
            pe.wait_ge(S("weights_loaded"), 16 * 3 * E)

            at_first = [pe.alloc_register(f"at_first{b}") for b in four]
            at_last = [pe.alloc_register(f"at_last{b}") for b in four]

            def load_places(regs, i, b):
                pe.load(regs, tab[0:1, bass.ds(U * i + b + BLOCKS, 4)])

            def block_step(i, b, start, first, ticketing, middle, last):
                if start:
                    pe.wait_ge(S("block_loaded", b), 16 * i + 16)
                    after(pe, "xT_ready", i, b, 2)
                    transpose(ps_xT[b % 2][:, 0:P], xblk[b][:, 0:D]).then_inc(S("xT_done"), 1)
                if first:
                    fb = item(i, b, 1)[1]
                    o = pe.snap(at_first[fb % 4], min_val=0, max_val=(E - 1) * WE)
                    after(pe, "xT_ready", i, b, 1)
                    after(pe, "hid_ready", i, b, 3)
                    mm(ps_h[fb % 2][:, :], xT[fb % 2][:, :], weights[:, bass.ds(o, 2 * H)], start=True,
                       stop=True).then_inc(S("h_done"), 1)
                if start and b % 4 == 0:
                    load_places(at_first, i, b)
                if middle:
                    mb = item(i, b, 3)[1]
                    after(pe, "hid_ready", i, b, 3)
                    after(pe, "hidT_ready", i, b, 5)
                    for c in two:
                        m = transpose(ps_hT[mb % 2][:, c * P:(c + 1) * P], hid[mb % 2][:, c * P:(c + 1) * P])
                    m.then_inc(S("hidT_done"), 1)
                if last:
                    lb = item(i, b, 4)[1]
                    o = pe.snap(at_last[lb % 4], min_val=0, max_val=(E - 1) * WE)
                    after(pe, "hidT_ready", i, b, 4)
                    after(pe, "y_ready", i, b, 6)
                    for c in two:
                        m = mm(ps_y[lb % 2][:, 0:D], hidT[lb % 2][:, c * P:(c + 1) * P],
                               weights[:, bass.ds(o + (2 * H + c * D), D)], start=(c == 0), stop=(c == 1))
                    m.then_inc(S("y_done"), 1)
                if start and b % 4 == 3:
                    load_places(at_last, i, b - 3)

            block_pipeline(pe, block_step)


_INPUTS = ["x", "adj", "wt", "gnn_b", "gate_w", "gate_b", "w1", "w2", "w3"]


def kernel(x, adj, L0_gnn_W, L0_gnn_b, L0_ffn_gate_w, L0_ffn_gate_b, L0_ffn_w1, L0_ffn_w2, L0_ffn_w3):
    import concourse.bacc as bacc
    from concourse.bass_utils import run_bass_kernel_spmd

    x, adj = np.asarray(x), np.asarray(adj)
    n = x.shape[0]
    T = -(-n // P)
    T += T % 2
    pad = T * P - n
    xt = np.pad(x, ((0, pad), (0, 0)), mode="edge").reshape(T, P, D).transpose(1, 0, 2).reshape(P, T * D)
    a = np.pad(np.pad(adj, ((0, pad), (0, 0)), mode="edge"), ((0, 0), (0, pad)))
    a = a.reshape(T, P, T, P).transpose(0, 3, 2, 1).reshape(T, P, T * P)
    arrays = dict(x=xt, adj=a, wt=np.asarray(L0_gnn_W).T, gnn_b=L0_gnn_b, gate_w=L0_ffn_gate_w,
                  gate_b=L0_ffn_gate_b, w1=L0_ffn_w1, w2=L0_ffn_w2, w3=L0_ffn_w3)
    arrays = {k: np.ascontiguousarray(v) for k, v in arrays.items()}
    nc = bacc.Bacc("TRN2", target_bir_lowering=False, num_devices=1)
    aps = [nc.dram_tensor(k, arrays[k].shape, mybir.dt.from_np(arrays[k].dtype), kind="ExternalInput").ap()
           for k in _INPUTS]
    out = nc.dram_tensor("out", (n, D), mybir.dt.float32, kind="ExternalOutput").ap()
    adj_ffn(nc, *aps, out)
    r = run_bass_kernel_spmd(nc, [arrays], core_ids=[0])
    return r.results[0]["out"]
```

```python
from contextlib import ExitStack

import numpy as np
import concourse.bass as bass
from concourse import mybir

P = 128
D = 128
E = 16
H = 256
EPS = 1e-5
XSCALE = 4096.0
XPW = 264
ROW = 132
DEST, WEIGHT = 128, 129
NOWHERE = 1 << 20
ROUNDER = 12582912.0
JH = 2
U = 8
WE = 3 * H


def adj_ffn(nc, x, adj, wt, gnn_b, gate_w, gate_b, w1, w2, w3, out):
    f32, f16, bf16, i32, u32 = (mybir.dt.float32, mybir.dt.float16, mybir.dt.bfloat16,
                                mybir.dt.int32, mybir.dt.uint32)
    ALU, ACT, AX = mybir.AluOpType, mybir.ActivationFunctionType, mybir.AxisListType

    T = x.shape[1] // D
    JT = T // JH
    PAIRS = T // 2
    HALVES = [(0, JT), (JT, T)]
    BOUND = T * P * 2 - 1
    BLOCKS = (T * P * 2 + E * (P - 1)) // P
    RUN = BLOCKS
    BLOCKS += -BLOCKS % 4
    REGION = T * P + P
    LISTED = PAIRS - 3
    EARLY = (LISTED * 4 * P - E * (P - 1)) // P // U * U
    TRASH = E * REGION
    DUMMY = TRASH + P
    ROWS = DUMMY + P
    FILL_FROM = U + 1
    n_tokens = out.shape[0]
    CHUNKS = [(a, min(a + 7, T)) for a in range(0, T, 7)]
    CONSTS = 20

    routed = nc.dram_tensor("routed_rows", [ROWS, ROW], f32).ap()
    returned = nc.dram_tensor("returned_rows", [T * P * 2, D], f32).ap()

    ctx = ExitStack()
    with ctx:
        def sb(name, shape, dt):
            return ctx.enter_context(nc.sbuf_tensor(name, shape, dt))

        def bank(name):
            return ctx.enter_context(nc.psum_tensor(name, [P, 512], f32))

        sems = {}

        BY_BUFFER = {"adj_loaded", "converted", "agg_done", "routed", "block_loaded", "x_loaded",
                      "y_returned", "back_loaded",
                     "m_ready", "m2_ready", "v_ready", "rstd0_ready", "rstd1_ready", "stats_ready", "xn_ready",
                     "xp_high", "xp_ready"}

        def S(name, b=""):
            key = f"{name}{b}" if name in BY_BUFFER else name
            if key not in sems:
                sems[key] = ctx.enter_context(nc.semaphore(key))
            return sems[key]

        x_in = sb("x_in", [P, T, D], f32)
        weights = sb("weights", [P, E * WE], f32)
        wt_s = sb("wt_s", [P, D], f32)
        gw_s = sb("gw_s", [P, E], f32)
        gb_s = sb("gb_s", [P, E], f32)
        b_rows = sb("b_rows", [P, D], f32)
        ident = sb("ident", [P, P], f32)
        tri = sb("tri", [P, P], bf16)
        ones = sb("ones", [P, P], bf16)
        onesf = sb("onesf", [P, P], f32)
        tri16 = sb("tri16", [E, E], f32)
        iota_e = sb("iota_e", [P, E], f32)
        base_tok = sb("base_tok", [P, E], f32)
        trash = sb("trash", [P, 1], f32)
        exponent = sb("exponent", [P, T], f32)
        e_col = sb("e_col", [E, 1], f32)
        base_col = sb("base_col", [E, 1], f32)
        iota_n = sb("iota_n", [E, BLOCKS], f32)
        iota_n128 = sb("iota_n128", [E, BLOCKS], f32)
        region_row = sb("region_row", [1, E], f32)
        filler = sb("filler", [P, ROW], f32)
        stats = sb("stats", [P, T, 6], f32)
        m_sum = sb("m_sum", [P, T], f32)
        m_dif = sb("m_dif", [P, T], f32)
        m_dif2 = sb("m_dif2", [P, T], f32)
        v_sum = sb("v_sum", [P, T], f32)
        v_eps = sb("v_eps", [P, T], f32)
        v_all = sb("v_all", [P, T], f32)
        mean1 = sb("mean1", [P, T], f32)
        rstd0 = sb("rstd0", [P, T], f32)
        rstd1 = sb("rstd1", [P, T], f32)
        xn = sb("xn", [P, T, D], f32)
        xp = sb("xp", [P, T, XPW], f16)
        two = range(2)
        adj_all = sb("adj_all", [P, 2 * T * P], i32)
        adj32 = [[adj_all[:, (b * JH + h) * JT * P:(b * JH + h + 1) * JT * P] for h in range(JH)] for b in two]
        a16 = [[sb(f"a16_{c}{b}", [P, T * P], f16) for b in two] for c in two]
        rdeg = sb("rdeg", [P, 2], f32)
        lo_part = sb("lo_part", [P, 2, D], f32)
        agg = sb("agg", [P, 2, D], f32)
        aggT = sb("aggT", [P, 2, D], f32)
        x1 = sb("x1", [P, T, D], f32)
        st2 = sb("st2", [P, 2, 6], f32)
        mv2 = sb("mv2", [P, 2, 2], f32)
        ve2 = sb("ve2", [P, 2], f32)
        rstd2 = sb("rstd2", [P, 2], f32)
        yn = sb("yn", [P, 2, D], f32)
        ynT = sb("ynT", [P, 2, D], f32)
        row = [sb(f"row{c}", [P, 2, 2, ROW], f32) for c in two]
        logits = sb("logits", [P, 2, E], f32)
        neg_max = sb("neg_max", [P, 2], f32)
        shifted = sb("shifted", [P, 2, E], f32)
        expo = sb("expo", [P, 2, E], f32)
        exp_sum = sb("exp_sum", [P, 2], f32)
        rsum = sb("rsum", [P, 2], f32)
        valid = sb("valid", [P, 2], f32)
        probs = sb("probs", [P, 2, E], f32)
        top8 = sb("top8", [P, 2, 8], f32)
        idx8 = sb("idx8", [P, 2, 8], u32)
        choice = sb("choice", [P, 2, 2], f32)
        den = sb("den", [P, 2], f32)
        rden = sb("rden", [P, 2], f32)
        onehot = sb("onehot", [P, 2, 2, E], f32)
        mask = sb("mask", [P, 2, E], bf16)
        mask_sum = sb("mask_sum", [P, E], bf16)
        place = sb("place", [P, 2, E], f32)
        picked = sb("picked", [P, 2, 2, E], f32)
        posf = sb("posf", [P, 4], f32)
        pos = [sb(f"pos{c}", [P, 4], i32) for c in two]
        full0 = sb("full0", [E, 1], f32)
        full = sb("full", [E, 1], f32)
        listed = sb("listed", [E, 1], f32)
        new = sb("new", [E, 1], f32)
        seq = sb("seq", [E, 1], f32)
        end = sb("end", [E, 1], f32)
        lag = sb("lag", [E, 1], f32)
        off = sb("off", [E, 1], f32)
        past = sb("past", [E, BLOCKS], f32)
        holds = sb("holds", [E, BLOCKS], f32)
        offs = sb("offs", [E, BLOCKS], f32)
        tabf = sb("tabf", [1, 2 * BLOCKS], f32)
        tab = sb("tab", [1, 2 * BLOCKS], i32)
        endf = sb("endf", [1, E], f32)
        endi = sb("endi", [1, E], i32)
        four, turn = range(4), range(U)
        xblk = [sb(f"xblk{b}", [P, ROW], f32) for b in turn]
        ticket = [sb(f"ticket{b}", [P, 2], f32) for b in turn]
        xT = [sb(f"xT{b}", [P, P], f32) for b in two]
        th = [sb(f"th{b}", [P, H], f32) for b in two]
        gated = [sb(f"gated{b}", [P, H], f32) for b in two]
        hid = [sb(f"hid{b}", [P, H], f32) for b in two]
        hidT = [sb(f"hidT{b}", [P, H], f32) for b in two]
        yblk = [sb(f"yblk{b}", [P, D], f32) for b in turn]
        back = adj_all[:, :].bitcast(f32).rearrange("p (t d) -> p t d", d=2 * D)

        psA = [[bank(f"psA{c}{b}") for b in two] for c in two]
        psTG, psLR = bank("psTG"), bank("psLR")
        psT, psG, psL, psR = psTG[:, 0:2 * D], psTG[:, 2 * D:4 * D], psLR[:, 0:2 * E], psLR[:, 2 * E:4 * E]
        psX, psY = bank("psX"), bank("psY")
        ps_h, ps_hT, ps_xT, ps_y = psA[1], psA[0], psX, [psY, psTG]
        ps_list = [psX, psLR]

        block = ctx.enter_context(nc.Block())

        def item(i, b, back):
            return (i, b - back) if b >= back else item(i - 1, b + U, back)

        def after(eng, name, i, b, back=0):
            i, b = item(i, b, back)
            if not (isinstance(i, int) and i < 0):
                eng.wait_ge(S(name, b), i + 1 if name in BY_BUFFER else U * i + b + 1)

        def since(eng, name, s, back, b=""):
            if not (isinstance(s, int) and s < back):
                eng.wait_ge(S(name, b), s - back + 1)

        def routed_before(eng, n, s, back):
            if not (isinstance(s, int) and s < back):
                eng.wait_ge(S("routed", n), 16 * (s - back) + 16)

        def apart(eng):
            eng.nop(nofuse=True)

        def pipelines(eng, tile_step, block_step, list_part=lambda k, part: None, list_places=(0, 1, 2),
                      before_blocks=lambda: None):
            def tiles(s, c, between=lambda k: None):
                on = [True] * 4 if not isinstance(s, int) else [0 <= s - back < PAIRS for back in range(4)]
                tile_step(s, c, between, *on)

            def blocks(i, b):
                s = U * i + b if isinstance(i, int) else None
                if s == 0:
                    before_blocks()
                on = [s is None or 0 <= s - back < RUN for back in range(5)]
                block_step(i, b, *on)

            turns = (PAIRS - 5) // 2
            for s in range(5):
                tiles(s, s % 2)
            with eng.Fori(0, turns) as i:
                tiles(2 * i + 5, 1)
                tiles(2 * i + 6, 0)
            for s in range(5 + 2 * turns, PAIRS):
                tiles(s, s % 2)
            tiles(PAIRS, PAIRS % 2, lambda k: k in list_places and list_part(0, list_places.index(k)))
            tiles(PAIRS + 1, (PAIRS + 1) % 2, lambda k: k == 6 and blocks(0, 0))
            tiles(PAIRS + 2, PAIRS % 2, lambda k: k in (2, 4) and blocks(0, k // 2))
            for n in range(3, EARLY):
                list_part(1, n - 3)
                blocks(n // U, n % U)
            with eng.Fori(EARLY // U, RUN // U) as i:
                for b in turn:
                    blocks(i, b)
            for s in range(RUN // U * U, RUN + 4):
                blocks(s // U, s % U)

        LISTS = [(0, EARLY), (EARLY, BLOCKS)]

        def of_list(tensor, k):
            a, z = LISTS[k]
            return tensor[:, :].rearrange("p (w n) -> p w n", w=2)[:, :, a:z]

        def load_weights(eng, e):
            per_expert = weights[:, :].rearrange("p (e n) -> p e n", n=WE)
            sources = [w.rearrange("e p n -> p e n") for w in (w1, w2, w3[:, 0:P, :], w3[:, P:H, :])]
            for w, o in zip(sources, (0, H, 2 * H, 2 * H + D)):
                eng.dma_start(per_expert[:, e:e + 4, o:o + w.shape[2]], w[:, e:e + 4, :])\
                    .then_inc(S("weights_loaded"), 16)

        @block.sync
        def _(sp):
            for k, (a, z) in enumerate(HALVES):
                sp.dma_start(x_in[:, a:z, :], x.rearrange("p (t d) -> p t d", d=D)[:, a:z, :])\
                    .then_inc(S("x_loaded", k), 16)

            def load_adjacency(i):
                for b in two:
                    for h in range(JH):
                        if not isinstance(i, int):
                            sp.wait_ge(S("converted", f"{b}{h}"), i)
                        sp.dma_start(adj32[b][h], adj[2 * i + b, :, h * JT * P:(h + 1) * JT * P])\
                            .then_inc(S("adj_loaded", f"{b}{h}"), 16)

            load_adjacency(0)
            sp.dma_start(b_rows[:, :], gnn_b.partition_broadcast(P)).then_inc(S("b_loaded"), 16)
            sp.dma_start(wt_s[:, :], wt).then_inc(S("wt_loaded"), 16)
            sp.dma_start(gw_s[:, :], gate_w).then_inc(S("gw_loaded"), 16)
            sp.dma_start(gb_s[:, :], gate_b.partition_broadcast(P)).then_inc(S("gb_loaded"), 16)

            with sp.Fori(1, PAIRS) as i:
                load_adjacency(i)
            load_weights(sp, 4)
            for n in range(4):
                routed_before(sp, n, PAIRS - 5, 0)
            load_weights(sp, 8)
            sp.wait_ge(S("rstd2_ready"), PAIRS - 1)
            load_weights(sp, 12)

            def load_blocks(i, buffers=turn):
                for b in buffers:
                    first = sp.value_load(tab[0:1, bass.ds(U * i + b, 1)], min_val=0, max_val=DUMMY)
                    after(sp, "xT_done", i, b, U)
                    after(sp, "ticket_ready", i, b, U)
                    sp.dma_start(xblk[b][:, :], routed[bass.ds(first, P), :]).then_inc(S("block_loaded", b), 16)

            ends = [sp.alloc_register(f"end{k}") for k in range(4)]

            def fill_tail(e):
                if e == 0:
                    sp.wait_ge(S("ends_ready"), 1)
                    sp.wait_ge(S("filler_ready"), 1)
                if e % 4 == 0:
                    sp.load(ends, endi[0:1, e:e + 4])
                end = sp.snap(ends[e % 4], min_val=0, max_val=TRASH - P)
                sp.dma_start(routed[bass.ds(end, P), :], filler[:, :]).then_inc(S("tails_filled"), 16)

            sp.wait_ge(S("tab_ready"), 1)
            sp.wait_ge(S("dummy_filled"), 16)
            for n in range(4):
                routed_before(sp, n, LISTED - 1, 0)
            for n in range(EARLY):
                load_blocks(n // U, [n % U])
                if n >= FILL_FROM:
                    fill_tail(n - FILL_FROM)
            for e in range(EARLY - FILL_FROM, E):
                fill_tail(e)
            sp.wait_ge(S("tab_ready"), 2)
            sp.wait_ge(S("tails_filled"), 16 * E)
            for n in range(4):
                routed_before(sp, n, PAIRS - 1, 0)
            with sp.Fori(EARLY // U, RUN // U) as i:
                load_blocks(i)
            load_blocks(RUN // U, range(RUN % U))
            for b in turn:
                sp.wait_ge(S("y_returned", b), 16 * len(range(b, RUN, U)))
            pairs = returned.rearrange("(t p k) d -> p t (k d)", p=P, k=2)
            for c, (a, z) in enumerate(CHUNKS):
                sp.dma_start(back[:, a:z, :], pairs[:, a:z, :]).then_inc(S("back_loaded", c), 16)
            whole = n_tokens // P
            for c, (a, z) in enumerate(CHUNKS):
                sp.wait_ge(S("combined"), c + 1)
                z = min(z, whole)
                sp.dma_start(out[a * P:z * P, :].rearrange("(t p) d -> p t d", p=P), xn[:, a:z, :])\
                    .then_inc(S("out_stored"), 16)
            left = n_tokens - whole * P
            sp.dma_start(out[whole * P:n_tokens, :], xn[0:left, whole, :]).then_inc(S("out_stored"), 16)
            sp.wait_ge(S("out_stored"), 16 * (len(CHUNKS) + 1))

        @block.scalar
        def _(act):
            act.wait_ge(S("x_loaded", 0), 16)
            load_weights(act, 0)
            for k, (a, z) in enumerate(HALVES):
                act.wait_ge(S("xn_ready", k), 1)
                nc.scalar.activation(xp[:, a:z, 0:D], xn[:, a:z, :], ACT.Copy).then_inc(S("xp_high", k), 1)

            def step(s, c, between, convert, aggregate, front, route):
                if front:
                    since(act, "rdeg_ready", s, 2)
                    since(act, "agg_ready", s, 3)
                    for b in two:
                        last = nc.scalar.activation(lo_part[:, b, :], psA[c][b][:, D:2 * D], ACT.Copy,
                                                    scale=rdeg[:, b:b + 1])
                    last.then_inc(S("lo_ready"), 1)
                between(0)
                if route:
                    since(act, "shift_ready", s, 3)
                    since(act, "probs_ready", s, 4)
                    nc.scalar.activation(expo[:, :, :], shifted[:, :, :], ACT.Exp).then_inc(S("exp_ready"), 1)
                between(1)
                if front:
                    since(act, "aggT_done", s, 2)
                    since(act, "gnn_done", s, 3)
                    nc.scalar.activation(aggT[:, :, :], psT.rearrange("p (b d) -> p b d", b=2),
                                         ACT.Copy).then_inc(S("aggT_ready"), 1)
                if route:
                    since(act, "yn_ready", s, 3)
                    for n in range(4):
                        routed_before(act, n, s, 5)
                    for k in two:
                        last = nc.scalar.activation(row[1 - c][:, :, k, 0:D], yn[:, :, :], ACT.Copy)
                    last.then_inc(S("rows_ready"), 1)
                for k in range(2, 6):
                    between(k)
                if front:
                    since(act, "ynT_done", s, 2)
                    since(act, "logits_done", s, 3)
                    nc.scalar.activation(ynT[:, :, :], psT.rearrange("p (b d) -> p b d", b=2),
                                         ACT.Copy).then_inc(S("ynT_ready"), 1)
                between(6)
                between(7)

            def block_step(i, b, start, first, ticketing, middle, last):
                if start:
                    after(act, "xT_done", i, b, 0)
                    after(act, "h_done", i, b, 2)
                    nc.scalar.activation(xT[b % 2][:, :], ps_xT[:, 0:P], ACT.Copy).then_inc(S("xT_ready"), 1)
                if first:
                    fb = item(i, b, 1)[1]
                    after(act, "h_done", i, b, 1)
                    after(act, "hid_ready", i, b, 3)
                    nc.scalar.activation(th[fb % 2][:, :], ps_h[fb % 2][:, 0:H], ACT.Tanh, scale=0.5)\
                        .then_inc(S("th_ready"), 1)
                if middle:
                    mb = item(i, b, 3)[1]
                    after(act, "hidT_done", i, b, 3)
                    after(act, "y_done", i, b, 5)
                    nc.scalar.activation(hidT[mb % 2][:, :], ps_hT[mb % 2][:, 0:H], ACT.Copy)\
                        .then_inc(S("hidT_ready"), 1)
                if last:
                    lb = item(i, b, 4)[1]
                    after(act, "y_done", i, b, 4)
                    after(act, "ticket_ready", i, b, 4)
                    nc.scalar.activation(yblk[lb][:, :], ps_y[lb % 2][:, 0:D], ACT.Copy,
                                         scale=ticket[lb][:, 1:2]).then_inc(S("y_ready"), 1)

            pipelines(act, step, block_step)

        @block.gpsimd
        def _(pool):
            g = nc.gpsimd
            big = dict(allow_small_or_imprecise_dtypes=True)
            g.memset(exponent[:, :], -0.5).then_inc(S("exponent_ready"), 1)
            g.memset(ident[:, :], 0.0).then_inc(S("const_memset"), 1)
            g.memset(tri[:, :], 1.0).then_inc(S("const_memset"), 1)
            g.memset(tri16[:, :], 1.0).then_inc(S("const_memset"), 1)
            g.memset(filler[:, :], 0.0).then_inc(S("const_memset"), 1)
            for c in two:
                g.memset(row[c][:, :, :, :], 0.0).then_inc(S("const_memset"), 1)
            pool.wait_ge(S("const_memset"), 6)
            g.affine_select(out=ident[:, :], in_=ident[:, :], compare_op=ALU.not_equal, fill=1.0, base=0,
                            pattern=[[-1, P]], channel_multiplier=1).then_inc(S("const_ready"), 1)
            for m, n in ((tri, P), (tri16, E)):
                g.affine_select(out=m[:, :], in_=m[:, :], compare_op=ALU.is_gt, fill=0.0, base=0,
                                pattern=[[1, n]], channel_multiplier=-1).then_inc(S("const_ready"), 1)
            g.memset(filler[:, DEST:DEST + 1].bitcast(i32), NOWHERE).then_inc(S("filler_ready"), 1)
            for c in two:
                g.iota(row[c][:, :, :, DEST].bitcast(i32), pattern=[[2 * P, 2], [1, 2]], base=4 * P * c,
                       channel_multiplier=2).then_inc(S("const_ready"), 1)
            g.memset(ones[:, :], 1.0).then_inc(S("const_ready"), 1)
            g.memset(onesf[:, :], 1.0).then_inc(S("const_ready"), 1)
            g.memset(mask_sum[:, :], 0.0).then_inc(S("const_ready"), 1)
            g.memset(listed[:, :], 0.0).then_inc(S("const_ready"), 1)
            g.memset(tabf[:, 0:BLOCKS], float(DUMMY)).then_inc(S("const_ready"), 1)
            g.memset(tabf[:, BLOCKS:2 * BLOCKS], 0.0).then_inc(S("const_ready"), 1)
            g.memset(xp[:, :, 2 * D:2 * D + 1], XSCALE).then_inc(S("const_ready"), 1)
            g.iota(iota_e[:, :], pattern=[[1, E]], base=1, channel_multiplier=0, **big).then_inc(S("const_ready"), 1)
            g.iota(base_tok[:, :], pattern=[[REGION, E]], base=-TRASH, channel_multiplier=-1, **big)\
                .then_inc(S("const_ready"), 1)
            g.iota(trash[:, :], pattern=[[0, 1]], base=TRASH, channel_multiplier=1, **big)\
                .then_inc(S("const_ready"), 1)
            g.iota(e_col[:, :], pattern=[[0, 1]], base=0, channel_multiplier=WE, **big)\
                .then_inc(S("const_ready"), 1)
            g.iota(base_col[:, :], pattern=[[0, 1]], base=-DUMMY, channel_multiplier=REGION, **big)\
                .then_inc(S("const_ready"), 1)
            g.iota(iota_n[:, :], pattern=[[1, BLOCKS]], base=0, channel_multiplier=0, **big)\
                .then_inc(S("const_ready"), 1)
            g.iota(iota_n128[:, :], pattern=[[P, BLOCKS]], base=0, channel_multiplier=0, **big)\
                .then_inc(S("const_ready"), 1)
            g.iota(region_row[:, :], pattern=[[REGION, E]], base=0, channel_multiplier=0, **big)\
                .then_inc(S("const_ready"), 1)
            pool.wait_ge(S("filler_ready"), 1)
            pool.dma_start(routed[DUMMY:DUMMY + P, :], filler[:, :]).then_inc(S("dummy_filled"), 16)
            pool.wait_ge(S("exponent_ready"), 1)
            for k, (a, z) in enumerate(HALVES):
                pool.wait_ge(S("v_ready", k), 1)
                g.tensor_tensor(rstd0[:, a:z], v_all[:, a:z], exponent[:, a:z], ALU.pow)\
                    .then_inc(S("rstd0_ready", k), 1)
            pool.wait_ge(S("b_loaded"), 16)
            for k, (a, z) in enumerate(HALVES):
                pool.wait_ge(S("xn_ready", k), 1)
                g.tensor_tensor(x_in[:, a:z, :], x_in[:, a:z, :],
                                b_rows[:, None, :].broadcast_to([P, z - a, D]), ALU.add).then_inc(S("xb_ready"), 1)

            def step(s, c, between, convert, aggregate, front, route):
                early = isinstance(s, int) and s < 5
                for k in range(4):
                    between(k)
                if route and not early:
                    for n in range(4):
                        routed_before(pool, n, s, 5)
                    apart(pool)
                    dest = row[1 - c][:, :, :, DEST].bitcast(i32)
                    g.tensor_scalar(dest, dest, 8.0 * P, None, ALU.add).then_inc(S("dest_ready"), 1)
                between(4)
                if front:
                    since(pool, "ve_ready", s, 2)
                    since(pool, "yn_ready", s, 3)
                    g.tensor_tensor(rstd2[:, :], ve2[:, :], exponent[:, 0:2], ALU.pow)\
                        .then_inc(S("rstd2_ready"), 1)
                between(5)
                if route:
                    since(pool, "pos_ready", s, 3)
                    since(pool, "weight_ready", s, 3)
                    since(pool, "rows_ready", s, 3)
                    if not early:
                        pool.wait_ge(S("dest_ready"), s - 4)
                    for n in range(4):
                        routed_before(pool, n, s, 4)
                    apart(pool)
                    for n in range(4):
                        g.indirect_dma_start(routed[:, :], bass.IndirectOffsetOnAxis(pos[1 - c][:, n:n + 1], 0),
                                             row[1 - c][:, n // 2, n % 2, :], None).then_inc(S("routed", n), 16)
                between(6)
                between(7)

            pool.wait_ge(S("const_ready"), CONSTS)
            def block_step(i, b, start, first, ticketing, middle, last):
                if not (isinstance(i, int) and i == 0):
                    pool.wait_ge(S("y_returned", b), 16 * i)
                if ticketing:
                    ti, tb = item(i, b, 2)
                    pool.wait_ge(S("block_loaded", tb), 16 * ti + 16)
                    apart(pool)
                    g.tensor_copy(ticket[tb][:, :], xblk[tb][:, DEST:DEST + 2]).then_inc(S("ticket_ready"), 1)
                if last:
                    lb = item(i, b, 4)[1]
                    after(pool, "ticket_ready", i, b, 4)
                    after(pool, "y_ready", i, b, 4)
                    apart(pool)
                    g.indirect_dma_start(returned[:, :],
                                         bass.IndirectOffsetOnAxis(ticket[lb][:, 0:1].bitcast(i32), 0),
                                         yblk[lb][:, :], None, bounds_check=BOUND, oob_is_err=False)\
                        .then_inc(S("y_returned", lb), 16)

            pipelines(pool, step, block_step)

        @block.vector
        def _(dve):
            v = nc.vector

            def then(ins, name, b=""):
                ins.then_inc(S(name, b), 1)

            def convert_part(s, c, b, h):
                dve.wait_ge(S("adj_loaded", f"{b}{h}"), 16 * s + 16)
                since(dve, "agg_done", s, 2, b)
                v.tensor_scalar(a16[c][b][:, h * JT * P:(h + 1) * JT * P], adj32[b][h], 1.0, None,
                                ALU.is_equal).then_inc(S("converted", f"{b}{h}"), 1)

            def variances(k, a, z):
                dve.wait_ge(S("x_loaded", k), 16)
                for t in range(a, z):
                    last = v.bn_stats(stats[:, t, :], x_in[:, t, :])
                then(last, "stats_ready", k)
                dve.wait_ge(S("stats_ready", k), 1)
                then(v.tensor_tensor(m_sum[:, a:z], stats[:, a:z, 1], stats[:, a:z, 4], ALU.add), "m_ready", k)
                then(v.tensor_tensor(m_dif[:, a:z], stats[:, a:z, 1], stats[:, a:z, 4], ALU.subtract), "m_ready", k)
                then(v.tensor_tensor(v_sum[:, a:z], stats[:, a:z, 2], stats[:, a:z, 5], ALU.add), "m_ready", k)
                dve.wait_ge(S("m_ready", k), 3)
                then(v.tensor_scalar(mean1[:, a:z], m_sum[:, a:z], 0.5, None, ALU.mult), "m2_ready", k)
                then(v.tensor_tensor(m_dif2[:, a:z], m_dif[:, a:z], m_dif[:, a:z], ALU.mult), "m2_ready", k)
                then(v.tensor_scalar(v_eps[:, a:z], v_sum[:, a:z], 1.0 / D, EPS, ALU.mult, ALU.add), "m2_ready", k)
                dve.wait_ge(S("m2_ready", k), 3)
                then(v.scalar_tensor_tensor(v_all[:, a:z], m_dif2[:, a:z], 0.25, v_eps[:, a:z], ALU.mult, ALU.add),
                     "v_ready", k)

            def normalise(k, a, z):
                dve.wait_ge(S("rstd0_ready", k), 1)
                then(v.tensor_scalar(rstd1[:, a:z], rstd0[:, a:z], XSCALE, None, ALU.mult), "rstd1_ready", k)
                dve.wait_ge(S("rstd1_ready", k), 1)
                for t in range(a, z):
                    last = v.tensor_scalar(xn[:, t, :], x_in[:, t, :], mean1[:, t:t + 1], rstd1[:, t:t + 1],
                                           ALU.subtract, ALU.mult)
                then(last, "xn_ready", k)

            def low_part(k, a, z):
                dve.wait_ge(S("xn_ready", k), 1)
                dve.wait_ge(S("xp_high", k), 1)
                then(v.tensor_tensor(xp[:, a:z, D:2 * D], xn[:, a:z, :], xp[:, a:z, 0:D], ALU.subtract),
                     "xp_ready", k)

            variances(0, *HALVES[0])
            variances(1, *HALVES[1])
            normalise(0, *HALVES[0])
            convert_part(0, 0, 0, 0)
            low_part(0, *HALVES[0])
            convert_part(0, 0, 0, 1)
            normalise(1, *HALVES[1])
            convert_part(0, 0, 1, 0)
            low_part(1, *HALVES[1])
            convert_part(0, 0, 1, 1)
            dve.wait_ge(S("const_ready"), CONSTS)

            def step(s, c, between, convert, aggregate, front, route):
                if isinstance(s, int) and s == 0:
                    return
                def spread(ap):
                    return ap[:, :, None].broadcast_to([P, 2, E])

                if front:
                    since(dve, "agg_done", s, 2, 0)
                    since(dve, "agg_done", s, 2, 1)
                    since(dve, "agg_ready", s, 3)
                    for b in two:
                        last = v.reciprocal(rdeg[:, b:b + 1], psA[c][b][:, 2 * D:2 * D + 1])
                    then(last, "rdeg_ready")
                if convert:
                    convert_part(s, c, 0, 0)
                if route:
                    since(dve, "logits_done", s, 3)
                    if isinstance(s, int) and s == 3:
                        dve.wait_ge(S("gb_loaded"), 16)
                    since(dve, "shift_ready", s, 4)
                    then(v.tensor_tensor(logits[:, :, :], psL.rearrange("p (b e) -> p b e", b=2),
                                         gb_s[:, None, :].broadcast_to([P, 2, E]), ALU.add), "logits_ready")
                    since(dve, "logits_ready", s, 3)
                    then(v.tensor_reduce(neg_max[:, :], logits[:, :, :], axis=AX.X, op=ALU.max, negate=True), "max_ready")
                    since(dve, "max_ready", s, 3)
                    since(dve, "exp_ready", s, 4)
                    then(v.tensor_tensor(shifted[:, :, :], logits[:, :, :], spread(neg_max), ALU.add), "shift_ready")
                between(0)
                if front:
                    since(dve, "lo_ready", s, 2)
                    since(dve, "aggT_done", s, 3)
                    for b in two:
                        last = v.scalar_tensor_tensor(agg[:, b, :], psA[c][b][:, 0:D], rdeg[:, b:b + 1],
                                                      lo_part[:, b, :], ALU.mult, ALU.add)
                    then(last, "agg_ready")
                between(1)
                if route:
                    since(dve, "exp_ready", s, 3)
                    then(v.tensor_reduce(exp_sum[:, :], expo[:, :, :], axis=AX.X, op=ALU.add), "sum_ready")
                    since(dve, "sum_ready", s, 3)
                    then(v.reciprocal(rsum[:, :], exp_sum[:, :]), "rsum_ready")
                    v.tensor_scalar(valid[:, :], exp_sum[:, :], 0.5, None, ALU.is_ge).then_inc(S("valid_ready"), 1)
                    since(dve, "rsum_ready", s, 3)
                    then(v.tensor_tensor(probs[:, :, :], expo[:, :, :], spread(rsum), ALU.mult), "probs_ready")
                    since(dve, "probs_ready", s, 3)
                    apart(dve)
                    for b in two:
                        last = v.max(top8[:, b, :], probs[:, b, :])
                    then(last, "top_ready")
                    since(dve, "top_ready", s, 3)
                    then(v.tensor_tensor(den[:, :], top8[:, :, 0], top8[:, :, 1], ALU.add), "den_ready")
                    for b in two:
                        last = v.max_index(idx8[:, b, :], top8[:, b, :], probs[:, b, :])
                    then(last, "idx_ready")
                    since(dve, "den_ready", s, 3)
                    then(v.reciprocal(rden[:, :], den[:, :]), "rden_ready")
                    since(dve, "idx_ready", s, 3)
                    since(dve, "valid_ready", s, 3)
                    then(v.scalar_tensor_tensor(choice[:, :, :], idx8[:, :, 0:2], 1.0,
                                                valid[:, :, None].broadcast_to([P, 2, 2]), ALU.add, ALU.mult),
                         "choice_ready")
                    since(dve, "choice_ready", s, 3)
                    then(v.tensor_tensor(onehot[:, :, :, :],
                                         iota_e[:, None, None, :].broadcast_to([P, 2, 2, E]),
                                         choice[:, :, :, None].broadcast_to([P, 2, 2, E]), ALU.is_equal),
                         "onehot_ready")
                    since(dve, "onehot_ready", s, 3)
                    since(dve, "rank_done", s, 4)
                    since(dve, "mask_summed", s, 4)
                    then(v.tensor_tensor(mask[:, :, :], onehot[:, :, 0, :], onehot[:, :, 1, :], ALU.add),
                         "mask_ready")
                between(2)
                if convert:
                    convert_part(s, c, 0, 1)
                between(3)
                if front:
                    f = s - 2
                    since(dve, "gnn_done", s, 2)
                    if isinstance(s, int) and s == 2:
                        dve.wait_ge(S("xb_ready"), 2)
                    pair = slice(2 * f, 2 * f + 2) if isinstance(f, int) else bass.ds(2 * f, 2)
                    then(v.tensor_tensor(x1[:, pair, :], psG.rearrange("p (b d) -> p b d", b=2),
                                         x_in[:, pair, :], ALU.add), "x1_ready")
                if route:
                    since(dve, "rden_ready", s, 3)
                    for n in range(4):
                        routed_before(dve, n, s, 5)
                    then(v.scalar_tensor_tensor(row[1 - c][:, :, :, WEIGHT], top8[:, :, 0:2], 0.5,
                                                rden[:, :, None].broadcast_to([P, 2, 2]), ALU.mult, ALU.mult),
                         "weight_ready")
                    since(dve, "rank_done", s, 3)
                    then(v.tensor_tensor(place[:, :, :], psR[:, 0:2 * E].rearrange("p (b e) -> p b e", b=2),
                                         base_tok[:, None, :].broadcast_to([P, 2, E]), ALU.add), "place_ready")
                if front:
                    since(dve, "x1_ready", s, 2)
                    apart(dve)
                    for b in two:
                        last = v.bn_stats(st2[:, b, :], x1[:, 2 * f + b, :])
                    then(last, "st2_ready")
                if route:
                    if isinstance(s, int) and s == PAIRS:
                        dve.wait_ge(S("counts_done"), 1)
                    then(v.tensor_tensor(mask_sum[:, :], mask_sum[:, :], mask[:, 0, :], ALU.add), "mask_summed_0")
                    since(dve, "place_ready", s, 3)
                    then(v.tensor_tensor(picked[:, :, :, :], onehot[:, :, :, :],
                                         place[:, :, None, :].broadcast_to([P, 2, 2, E]), ALU.mult),
                         "picked_ready")
                if front:
                    since(dve, "st2_ready", s, 2)
                    apart(dve)
                    for b in two:
                        last = v.bn_aggr(mv2[:, b, :], st2[:, b, :])
                    then(last, "mv2_ready")
                if route:
                    since(dve, "picked_ready", s, 3)
                    then(v.tensor_reduce(posf[:, :], picked[:, :, :, :].rearrange("p b k e -> p (b k) e"),
                                         axis=AX.X, op=ALU.add), "posf_ready")
                if front:
                    since(dve, "mv2_ready", s, 2)
                    since(dve, "rstd2_ready", s, 3)
                    then(v.tensor_scalar(ve2[:, :], mv2[:, :, 1], EPS, None, ALU.add), "ve_ready")
                if route:
                    since(dve, "posf_ready", s, 3)
                    then(v.tensor_scalar(pos[1 - c][:, :], posf[:, :], trash[:, 0:1], None, ALU.add), "pos_ready")
                    since(dve, "mask_summed_0", s, 3)
                    then(v.tensor_tensor(mask_sum[:, :], mask_sum[:, :], mask[:, 1, :], ALU.add), "mask_summed")
                between(4)
                if convert:
                    convert_part(s, c, 1, 0)
                if front:
                    since(dve, "rstd2_ready", s, 2)
                    since(dve, "rows_ready", s, 3)
                    since(dve, "ynT_done", s, 3)
                    for b in two:
                        last = v.tensor_scalar(yn[:, b, :], x1[:, 2 * f + b, :], mv2[:, b, 0:1], rstd2[:, b:b + 1],
                                               ALU.subtract, ALU.mult)
                    then(last, "yn_ready")
                for k in range(5, U):
                    between(k)
                if convert:
                    convert_part(s, c, 1, 1)

            def list_part(k, part):
                a, z = LISTS[k]
                N = z - a
                ps = ps_list[k]
                if part == 0:
                    dve.wait_ge(S("counts_done"), k + 1)
                    half = (P - 1) / 2.0
                    then(v.tensor_scalar(full0[:, :], ps[0:E, 0:1], half if k else -half, 1.0 / P, ALU.add, ALU.mult),
                         "list_0")
                    if k:
                        then(v.tensor_tensor(endf[:, :], ps[0:1, 32:32 + E], region_row[:, :], ALU.add), "endf_ready")
                        dve.wait_ge(S("endf_ready"), 1)
                        then(v.tensor_copy(endi[:, :], endf[:, :]), "ends_ready")
                    dve.wait_ge(S("list_0"), k + 1)
                    then(v.tensor_scalar(full[:, :], full0[:, :], ROUNDER, ROUNDER, ALU.add, ALU.subtract), "list_1")
                    dve.wait_ge(S("list_1"), k + 1)
                    then(v.tensor_tensor(new[:, :], full[:, :], listed[:, :], ALU.subtract), "new_ready")
                    dve.wait_ge(S("new_ready"), k + 1)
                elif part == 1:
                    dve.wait_ge(S("seq_done"), k + 1)
                    then(v.tensor_copy(seq[:, :], ps[0:E, 0:1]), "list_2")
                    dve.wait_ge(S("list_2"), k + 1)
                    then(v.tensor_tensor(end[:, :], seq[:, :], new[:, :], ALU.add), "list_3")
                    then(v.tensor_tensor(lag[:, :], listed[:, :], seq[:, :], ALU.subtract), "list_3")
                    then(v.tensor_scalar(past[:, 0:N], iota_n[:, 0:N], seq[:, 0:1], None, ALU.is_ge), "list_3")
                    dve.wait_ge(S("list_3"), 3 * k + 3)
                    then(v.tensor_scalar(off[:, :], lag[:, :], float(P), base_col[:, 0:1], ALU.mult, ALU.add), "list_4")
                    then(v.scalar_tensor_tensor(holds[:, 0:N], iota_n[:, 0:N], end[:, 0:1], past[:, 0:N],
                                                ALU.is_lt, ALU.mult), "list_4")
                    dve.wait_ge(S("list_4"), 2 * k + 2)
                    then(v.scalar_tensor_tensor(offs[:, 0:N], iota_n128[:, 0:N], off[:, 0:1], holds[:, 0:N],
                                                ALU.add, ALU.mult), "offs_ready")
                    if k == 0:
                        then(v.tensor_reduce(listed[:, :], holds[:, 0:N], axis=AX.X, op=ALU.add), "listed_ready")
                        dve.wait_ge(S("listed_ready"), 1)
                elif part == 2:
                    dve.wait_ge(S("tab_done"), k + 1)
                    then(v.tensor_tensor(of_list(tabf, k), of_list(tabf, k),
                                         ps[0:1, 0:2 * N].rearrange("p (w n) -> p w n", w=2), ALU.add), "tabf_ready")
                    dve.wait_ge(S("tabf_ready"), k + 1)
                    then(v.tensor_copy(of_list(tab, k), of_list(tabf, k)), "tab_ready")

            def block_step(i, b, start, first, ticketing, middle, last):
                if first:
                    fb = item(i, b, 1)[1]
                    after(dve, "th_ready", i, b, 1)
                    after(dve, "hid_ready", i, b, 3)
                    then(v.scalar_tensor_tensor(gated[fb % 2][:, :], th[fb % 2][:, :], 1.0, ps_h[fb % 2][:, 0:H],
                                                ALU.add, ALU.mult), "gated_ready", fb)
                    after(dve, "gated_ready", i, b, 1)
                    after(dve, "hidT_done", i, b, 3)
                    then(v.tensor_tensor(hid[fb % 2][:, :], gated[fb % 2][:, :], ps_h[fb % 2][:, H:2 * H],
                                         ALU.mult), "hid_ready", fb)

            pipelines(dve, step, block_step, list_part, (1, 2, 4))

            for c, (a, z) in enumerate(CHUNKS):
                dve.wait_ge(S("back_loaded", c), 16)
                then(v.tensor_tensor(xn[:, a:z, :], back[:, a:z, 0:D], back[:, a:z, D:2 * D], ALU.add), "added")
                dve.wait_ge(S("added"), c + 1)
                then(v.tensor_tensor(xn[:, a:z, :], xn[:, a:z, :], x1[:, a:z, :], ALU.add), "combined")

        @block.tensor
        def _(pe):
            mm = nc.tensor.matmul

            def transpose(out_, in_):
                return nc.tensor.transpose(out_, in_, ident[:, :])

            pe.wait_ge(S("const_ready"), CONSTS)
            for name in ("wt_loaded", "gw_loaded"):
                pe.wait_ge(S(name), 16)

            def step(s, c, between, convert, aggregate, front, route):
                def aggregate_part(b, a, z):
                    if not aggregate:
                        return
                    if a == 0:
                        since(pe, "agg_ready", s, 3)
                    for j in range(a, z):
                        if j % JT == 0:
                            pe.wait_ge(S("converted", f"{b}{j // JT}"), s)
                            if isinstance(s, int) and s == 1:
                                pe.wait_ge(S("xp_high", j // JT), 1)
                                pe.wait_ge(S("xp_ready", j // JT), 1)
                        last = mm(psA[1 - c][b][:, 0:2 * D + 1], a16[1 - c][b][:, j * P:(j + 1) * P],
                                  xp[:, j, 0:2 * D + 1], start=(j == 0), stop=(j == T - 1))
                    if z == T:
                        last.then_inc(S("agg_done", b), 1)

                aggregate_part(0, 0, 6)
                if route:
                    since(pe, "ynT_ready", s, 3)
                    since(pe, "place_ready", s, 4)
                    for b in two:
                        o = psL[:, b * E:(b + 1) * E]
                        last = mm(o, ynT[:, b, :], gw_s[:, :], start=True, stop=True)
                    last.then_inc(S("logits_done"), 1)
                between(0)
                aggregate_part(0, 6, 18)
                if front:
                    since(pe, "agg_ready", s, 2)
                    since(pe, "ynT_ready", s, 3)
                    for b in two:
                        last = transpose(psT[:, b * D:(b + 1) * D], agg[:, b, :])
                    last.then_inc(S("aggT_done"), 1)
                between(1)
                between(2)
                aggregate_part(0, 18, T)
                if front:
                    since(pe, "aggT_ready", s, 2)
                    since(pe, "x1_ready", s, 3)
                    for b in two:
                        last = mm(psG[:, b * D:(b + 1) * D], aggT[:, b, :], wt_s[:, :], start=True, stop=True)
                    last.then_inc(S("gnn_done"), 1)
                between(3)
                aggregate_part(1, 0, 4)
                if route:
                    since(pe, "mask_ready", s, 3)
                    since(pe, "mask_summed", s, 4)
                    since(pe, "shift_ready", s, 3)
                    for b in two:
                        o = psR[:, b * E:(b + 1) * E]
                        mm(o, tri[:, :], mask[:, b, :], start=True, stop=False)
                        last = mm(o, ones[:, :], mask_sum[:, :], start=False, stop=(b == 0))
                    mm(o, ones[:, :], mask[:, 0, :], start=False, stop=True).then_inc(S("rank_done"), 1)
                between(4)
                aggregate_part(1, 4, T)
                if front:
                    since(pe, "yn_ready", s, 2)
                    for b in two:
                        last = transpose(psT[:, b * D:(b + 1) * D], yn[:, b, :])
                    last.then_inc(S("ynT_done"), 1)
                for k in range(5, U):
                    between(k)

            def list_part(k, part):
                a, z = LISTS[k]
                N = z - a
                ps = ps_list[k]
                if part == 0:
                    pe.wait_ge(S("mask_summed"), (LISTED, PAIRS)[k])
                    pe.wait_ge(S("place_ready"), (LISTED, PAIRS)[k])
                    m = mm(ps[0:E, 0:1], mask_sum[:, :], ones[:, 0:1], start=True, stop=True)
                    if k:
                        m = mm(ps[0:1, 32:32 + E], ones[:, 0:1], mask_sum[:, :], start=True, stop=True)
                    m.then_inc(S("counts_done"), 1)
                elif part == 1:
                    pe.wait_ge(S("new_ready"), k + 1)
                    if k:
                        pe.wait_ge(S("endf_ready"), 1)
                    mm(ps[0:E, 0:1], tri16[:, :], new[:, :], start=True, stop=True).then_inc(S("seq_done"), 1)
                elif part == 2:
                    pe.wait_ge(S("list_2"), k + 1)
                    pe.wait_ge(S("offs_ready"), k + 1)
                    mm(ps[0:1, 0:N], onesf[0:E, 0:1], offs[:, 0:N], start=True, stop=True)
                    mm(ps[0:1, N:2 * N], e_col[:, 0:1], holds[:, 0:N], start=True, stop=True)\
                        .then_inc(S("tab_done"), 1)

            def before_blocks():
                pe.wait_ge(S("tab_ready"), 1)
                pe.wait_ge(S("weights_loaded"), 16 * E)

            at_first = [pe.alloc_register(f"at_first{b}") for b in four]
            at_last = [pe.alloc_register(f"at_last{b}") for b in four]

            def load_places(regs, i, b):
                pe.load(regs, tab[0:1, bass.ds(U * i + b + BLOCKS, 4)])

            def block_step(i, b, start, first, ticketing, middle, last):
                if isinstance(i, int) and (i, b) == (EARLY // U - 1, U - 1):
                    pe.wait_ge(S("tab_ready"), 2)
                if start:
                    pe.wait_ge(S("block_loaded", b), 16 * i + 16)
                    after(pe, "xT_ready", i, b, 1)
                    transpose(ps_xT[:, 0:P], xblk[b][:, 0:D]).then_inc(S("xT_done"), 1)
                if first:
                    fb = item(i, b, 1)[1]
                    o = pe.snap(at_first[fb % 4], min_val=0, max_val=(E - 1) * WE)
                    after(pe, "xT_ready", i, b, 1)
                    after(pe, "hid_ready", i, b, 3)
                    mm(ps_h[fb % 2][:, :], xT[fb % 2][:, :], weights[:, bass.ds(o, 2 * H)], start=True,
                       stop=True).then_inc(S("h_done"), 1)
                if start and b % 4 == 0:
                    load_places(at_first, i, b)
                if middle:
                    mb = item(i, b, 3)[1]
                    after(pe, "hid_ready", i, b, 3)
                    after(pe, "hidT_ready", i, b, 5)
                    for c in two:
                        m = transpose(ps_hT[mb % 2][:, c * P:(c + 1) * P], hid[mb % 2][:, c * P:(c + 1) * P])
                    m.then_inc(S("hidT_done"), 1)
                if last:
                    lb = item(i, b, 4)[1]
                    o = pe.snap(at_last[lb % 4], min_val=0, max_val=(E - 1) * WE)
                    after(pe, "hidT_ready", i, b, 4)
                    after(pe, "y_ready", i, b, 6)
                    for c in two:
                        m = mm(ps_y[lb % 2][:, 0:D], hidT[lb % 2][:, c * P:(c + 1) * P],
                               weights[:, bass.ds(o + (2 * H + c * D), D)], start=(c == 0), stop=(c == 1))
                    m.then_inc(S("y_done"), 1)
                if b % 4 == 3:
                    load_places(at_last, i, b - 3)

            pipelines(pe, step, block_step, list_part, (0, 2, 3), before_blocks)


_INPUTS = ["x", "adj", "wt", "gnn_b", "gate_w", "gate_b", "w1", "w2", "w3"]


def kernel(x, adj, L0_gnn_W, L0_gnn_b, L0_ffn_gate_w, L0_ffn_gate_b, L0_ffn_w1, L0_ffn_w2, L0_ffn_w3):
    import concourse.bacc as bacc
    from concourse.bass_utils import run_bass_kernel_spmd

    x, adj = np.asarray(x), np.asarray(adj)
    n = x.shape[0]
    T = -(-n // P)
    T += T % 2
    pad = T * P - n
    xt = np.pad(x, ((0, pad), (0, 0)), mode="edge").reshape(T, P, D).transpose(1, 0, 2).reshape(P, T * D)
    a = np.pad(np.pad(adj, ((0, pad), (0, 0)), mode="edge"), ((0, 0), (0, pad)))
    a = a.reshape(T, P, T, P).transpose(0, 3, 2, 1).reshape(T, P, T * P)
    arrays = dict(x=xt, adj=a, wt=np.asarray(L0_gnn_W).T, gnn_b=L0_gnn_b, gate_w=L0_ffn_gate_w,
                  gate_b=L0_ffn_gate_b, w1=L0_ffn_w1, w2=L0_ffn_w2, w3=L0_ffn_w3)
    arrays = {k: np.ascontiguousarray(v) for k, v in arrays.items()}
    nc = bacc.Bacc("TRN2", target_bir_lowering=False, num_devices=1)
    aps = [nc.dram_tensor(k, arrays[k].shape, mybir.dt.from_np(arrays[k].dtype), kind="ExternalInput").ap()
           for k in _INPUTS]
    out = nc.dram_tensor("out", (n, D), mybir.dt.float32, kind="ExternalOutput").ap()
    adj_ffn(nc, *aps, out)
    r = run_bass_kernel_spmd(nc, [arrays], core_ids=[0])
    return r.results[0]["out"]
```
